# Optimizing a Trainium2 kernel written in Bass

```python
import numpy as np
import jax
import jax.numpy as jnp

def _softmax(x, axis=-1):
    return jax.nn.softmax(x, axis=axis)

def _gelu(x):
    return jax.nn.gelu(x, approximate=True)

def _silu(x):
    return jax.nn.silu(x)

def _sigmoid(x):
    return jax.nn.sigmoid(x)

def _layernorm(x, axis=-1, eps=1e-05):
    m = jnp.mean(x, axis=axis, keepdims=True)
    v = jnp.var(x, axis=axis, keepdims=True)
    return (x - m) / jnp.sqrt(v + eps)

def _scatter_add(tgt, idx, src, axis=0):
    return tgt.at[idx].add(src)

def _segment_sum(src, seg, n):
    return jax.ops.segment_sum(src, seg, n)
kernel_name = 'mk_gnn_resnorm_d1_gnn_r16_0762b3'

def setup_inputs(seed: int=0):
    np.random.seed(seed)
    _w = jnp.asarray

    def _rec_inputs():
        import jax
        import jax.numpy as jnp
        _gk = jax.random.key(seed)
        x = -0.0001538 + 1 * jax.random.normal(jax.random.fold_in(_gk, 1), (512, 768), jnp.float32)
        _s = jax.random.randint(jax.random.fold_in(_gk, 2), (8192,), 0, 512, jnp.int32)
        _d = jax.random.randint(jax.random.fold_in(_gk, 3), (8192,), 0, 512, jnp.int32)
        _loop = jnp.arange(512, dtype=jnp.int32)
        src = jnp.concatenate([_s, _d, _loop])
        dst = jnp.concatenate([_d, _s, _loop])
        _o = jnp.argsort(dst, stable=True)
        src = src[_o]
        dst = dst[_o]
        return (x, src, dst)
    x, src, dst = _rec_inputs()

    def _L0_gnn_setup():
        import jax, jax.numpy as jnp
        import numpy as np
        NEG_SLOPE = 0.2
        EPS = 1e-16
        N_NODES = 512
        N_EDGES = 4096
        D_IN = 768
        D_HID = 768
        H1 = 8
        H2 = 1

        def gat_layer(x, W, a_s, a_d, b, edge_index, concat):
            n = x.shape[0]
            H, C = a_s.shape
            h = (x @ W).reshape(n, H, C)
            src, dst = (edge_index[0], edge_index[1])
            alpha_s = jnp.einsum('nhc,hc->nh', h, a_s)
            alpha_d = jnp.einsum('nhc,hc->nh', h, a_d)
            e = jax.nn.leaky_relu(alpha_s[src] + alpha_d[dst], NEG_SLOPE)
            m = jax.ops.segment_max(e, dst, num_segments=n)
            e = jnp.exp(e - m[dst])
            denom = jax.ops.segment_sum(e, dst, num_segments=n)
            alpha = e / (denom[dst] + EPS)
            msg = h[src] * alpha[:, :, None]
            out = jax.ops.segment_sum(msg, dst, num_segments=n)
            out = out.reshape(n, H * C) if concat else out.mean(axis=1)
            return out + b
        key = jax.random.key(seed)
        ks = jax.random.split(key, 10)
        x = jax.random.normal(ks[0], (N_NODES, D_IN), dtype=jnp.float32)
        edge_list = jax.random.randint(ks[1], (2, N_EDGES), 0, N_NODES, dtype=jnp.int32)
        s = 0.05
        W1 = jax.random.normal(ks[2], (D_IN, H1 * D_HID), dtype=jnp.float32) * s
        a_src1 = jax.random.normal(ks[3], (H1, D_HID), dtype=jnp.float32) * s
        a_dst1 = jax.random.normal(ks[4], (H1, D_HID), dtype=jnp.float32) * s
        b1 = jnp.zeros((H1 * D_HID,), dtype=jnp.float32)
        W2 = jax.random.normal(ks[5], (H1 * D_HID, H2 * D_HID), dtype=jnp.float32) * s
        a_src2 = jax.random.normal(ks[6], (H2, D_HID), dtype=jnp.float32) * s
        a_dst2 = jax.random.normal(ks[7], (H2, D_HID), dtype=jnp.float32) * s
        b2 = jnp.zeros((H2 * D_HID,), dtype=jnp.float32)
        return {'x': x, 'W1': W1, 'a_src1': a_src1, 'a_dst1': a_dst1, 'b1': b1, 'W2': W2, 'a_src2': a_src2, 'a_dst2': a_dst2, 'b2': b2, 'edge_list': edge_list}
    _L0_gnn_all = _L0_gnn_setup()
    _L0_gnn_in = {k: v for k, v in _L0_gnn_all.items() if k in ('W1', 'a_src1', 'a_dst1', 'b1', 'W2', 'a_src2', 'a_dst2', 'b2')}
    del _L0_gnn_all
    return {'x': x, 'src': src, 'dst': dst, 'L0_gnn_W1': _L0_gnn_in['W1'], 'L0_gnn_a_src1': _L0_gnn_in['a_src1'], 'L0_gnn_a_dst1': _L0_gnn_in['a_dst1'], 'L0_gnn_b1': _L0_gnn_in['b1'], 'L0_gnn_W2': _L0_gnn_in['W2'], 'L0_gnn_a_src2': _L0_gnn_in['a_src2'], 'L0_gnn_a_dst2': _L0_gnn_in['a_dst2'], 'L0_gnn_b2': _L0_gnn_in['b2']}

def reference(x, src, dst, L0_gnn_W1, L0_gnn_a_src1, L0_gnn_a_dst1, L0_gnn_b1, L0_gnn_W2, L0_gnn_a_src2, L0_gnn_a_dst2, L0_gnn_b2):
    import jax
    import jax.numpy as jnp

    def _L0_gnn_ref(x, W1, a_src1, a_dst1, b1, W2, a_src2, a_dst2, b2, edge_list):
        import jax, jax.numpy as jnp
        import numpy as np
        NEG_SLOPE = 0.2
        EPS = 1e-16
        N_NODES = 512
        N_EDGES = 4096
        D_IN = 768
        D_HID = 768
        H1 = 8
        H2 = 1

        def gat_layer(x, W, a_s, a_d, b, edge_index, concat):
            n = x.shape[0]
            H, C = a_s.shape
            h = (x @ W).reshape(n, H, C)
            src, dst = (edge_index[0], edge_index[1])
            alpha_s = jnp.einsum('nhc,hc->nh', h, a_s)
            alpha_d = jnp.einsum('nhc,hc->nh', h, a_d)
            e = jax.nn.leaky_relu(alpha_s[src] + alpha_d[dst], NEG_SLOPE)
            m = jax.ops.segment_max(e, dst, num_segments=n)
            e = jnp.exp(e - m[dst])
            denom = jax.ops.segment_sum(e, dst, num_segments=n)
            alpha = e / (denom[dst] + EPS)
            msg = h[src] * alpha[:, :, None]
            out = jax.ops.segment_sum(msg, dst, num_segments=n)
            out = out.reshape(n, H * C) if concat else out.mean(axis=1)
            return out + b
        h = gat_layer(x, W1, a_src1, a_dst1, b1, edge_list, concat=True)
        h = jax.nn.elu(h)
        out = gat_layer(h, W2, a_src2, a_dst2, b2, edge_list, concat=True)
        return out
    edge_index = jnp.stack([src, dst])
    x = _layernorm(x + _L0_gnn_ref(x, L0_gnn_W1, L0_gnn_a_src1, L0_gnn_a_dst1, L0_gnn_b1, L0_gnn_W2, L0_gnn_a_src2, L0_gnn_a_dst2, L0_gnn_b2, edge_index), axis=-1)
    return x

_drawn_inputs = setup_inputs


def setup_inputs(seed=0):
    import zlib

    import numpy as np

    out = dict(_drawn_inputs(seed))
    spreads = {'L0_gnn_b1': (0.0, 0.1), 'L0_gnn_b2': (0.0, 0.1)}
    factors = {}
    for name, (base, spread) in spreads.items():
        noise = np.random.default_rng([zlib.crc32(name.encode()), seed]).standard_normal(out[name].shape)
        drawn = base * np.exp(spread * noise) if base else spread * noise
        out[name] = jnp.asarray(drawn.astype(out[name].dtype))
    for name, factor in factors.items():
        out[name] = (out[name] * factor).astype(out[name].dtype)
    return out
```

```python
import concourse.bass as bass
from concourse import mybir
from contextlib import ExitStack


def gat_resnorm_kernel(nc, x, xT, src, dst, W1, as1, ad1, b1c, W2, as2, ad2, b2, out):
    f32, f32r, bf16 = mybir.dt.float32, mybir.dt.float32r, mybir.dt.bfloat16
    i32, f16 = mybir.dt.int32, mybir.dt.float16
    ALU, ACT = mybir.AluOpType, mybir.ActivationFunctionType

    N, D, H, E = 512, 768, 8, 16896
    NT, FT = N // 128, D // 128
    HALF = D // 2
    EJ = E // 128
    GROUPS = [27, 27, 26, 26, 26]
    OHR = 8
    FIELD = 4096
    SLOPE, EPS, LN_EPS, BIG = 0.2, 1e-16, 1e-5, 1e30
    NR, N2 = 5, 3

    queue = {"sp": [], "act": [], "dve": [], "pool": [], "pe": []}
    count, seen = {}, {}
    ctx = ExitStack()
    with ctx:
        def sem(name):
            s = ctx.enter_context(nc.semaphore(name))
            count[name] = 0
            return (name, s)

        def put(eng, waits, fn, done=None, by=1):
            for w in waits:
                if w is None:
                    continue
                (name, s), v = w
                if seen.get((eng, name), 0) < v:
                    seen[eng, name] = v
                    queue[eng].append(lambda e, s=s, v=v: e.wait_ge(s, v))
            if done is None:
                queue[eng].append(lambda e: fn())
                return None
            count[done[0]] += by
            queue[eng].append(lambda e: fn().then_inc(done[1], by))
            return (done, count[done[0]])

        def sb(name, shape, dt, where=ctx):
            return where.enter_context(nc.sbuf_tensor(name, shape, dt))

        V, A, G, T, S = nc.vector, nc.scalar, nc.gpsimd, nc.tensor, nc.sync

        xTh = sb("xTh", [128, FT, N], f32r)
        xTl = sb("xTl", [128, FT, N], f32r)
        CT = sb("CT", [128, NT, N], f32)
        Mk = sb("Mk", [128, NT, N], bf16)
        Wr = sb("Wr", [128, NR, D], f32)
        W2h = sb("W2h", [128, N2, D], f32r)
        W2l = sb("W2l", [128, N2, D], f32r)
        h32 = sb("h32", [128, 2, D], f32)
        hh = sb("hh", [128, NT, D], f32r)
        hl = sb("hl", [128, NT, D], f32r)
        abc = sb("abc", [128, 2, 2, D], f32)
        rb = sb("rb", [128, N], f32)
        idn = sb("idn", [128, 128], f32)
        oner = sb("oner", [128, 128], f32r)
        b1s = sb("b1s", [128, H * FT], f32)
        asd = sb("asd", [128, 2, 2, NT], f32)
        amx = sb("amx", [128, NT], f32)
        zm = sb("zm", [128, NT], f32)
        mc = sb("mc", [128, NT], f32)
        junk = sb("junk", [128, D], bf16)
        with ExitStack() as c1:
            W1h = sb("W1h", [128, FT, D], f32r, c1)
            W1l = sb("W1l", [128, FT, D], f32r, c1)
        c2 = ctx.enter_context(ExitStack())
        xr = sb("xr", [128, NT, D], f32, c2)
        res = sb("res", [128, NT, D], f32, c2)
        b2b = sb("b2b", [128, D], f32, c2)
        a2b = sb("a2b", [128, 2, D], f32, c2)
        st6 = sb("st6", [128, NT, 2, 6], f32, c2)
        mv = sb("mv", [128, NT, 2], f32, c2)
        rs = sb("rs", [128, NT, 2], f32, c2)
        dn = sb("dn", [128, NT, 2], f32, c2)
        sb("pad", [128, 9216 - (2 * NT * D + 3 * D + NT * 12 + 3 * NT * 2)], f32, c2)
        with ExitStack() as c3:
            xTr = sb("xTr", [128, FT, N], f32, c3)
            si = sb("si", [128, EJ], i32, c3)
            di = sb("di", [128, EJ], i32, c3)
            t1 = sb("t1", [128, EJ], i32, c3)
            t2 = sb("t2", [128, EJ], i32, c3)
            t3 = sb("t3", [128, EJ], i32, c3)
            df = sb("df", [128, EJ], f32, c3)
            uf = sb("uf", [128, EJ], f32, c3)
            wf = sb("wf", [128, EJ], f32, c3)
            ioi = sb("ioi", [128, N], i32, c3)
            iof = sb("iof", [128, N], f16, c3)
            ohd = sb("ohd", [128, OHR, N], bf16, c3)
            ohs = sb("ohs", [128, OHR, 256], bf16, c3)
            ji = sb("ji", [128, 2, 2, N], i32, c3)
            jf = sb("jf", [128, 2, 2, N], i32, c3)
            cnt = sb("cnt", [128, 2, 2, N], i32, c3)
        L = sb("L", [128, NT, N], f32)
        Ph = sb("Ph", [128, NT, N], f32r)
        Pl = sb("Pl", [128, NT, N], f32r)
        y = sb("y", [128, 2, N], f32)
        ex = sb("ex", [128, 2, N], f32)
        gh = sb("gh", [128, FT, N], f32r)
        gl = sb("gl", [128, FT, N], f32r)

        O = [ctx.enter_context(nc.psum_tensor(f"O{i}", [128, 512], f32)) for i in range(6)]
        R = [ctx.enter_context(nc.psum_tensor(f"R{i}", [128, 512], f32)) for i in range(2)]

        def Ocols(t):
            return [(O[t][:, 0:512], 0, 512), (O[4 + t // 2][:, 256 * (t % 2):256 * (t % 2) + 256], 512, 768)]

        ring = {"k": 0, "rel": [None, None]}

        def bank():
            k = ring["k"] % 2
            ring["k"] += 1
            return k, R[k], ring["rel"][k]

        s_edge, s_xT, s_b1, s_out = sem("s_edge"), sem("s_xT"), sem("s_b1"), sem("s_out")
        s_edg2 = sem("s_edg2")
        s_wr = [sem(f"s_wr{i}") for i in range(NR)]
        s_abc = [sem(f"s_abc{i}") for i in range(4)]
        s_xr, s_b2, s_a2 = sem("s_xr"), sem("s_b2"), [sem("s_a20"), sem("s_a21")]
        s_io, s_cst, s_iof, s_key = sem("s_io"), sem("s_cst"), sem("s_iof"), sem("s_key")
        s_oh, s_hist, s_ji, s_jf, s_cnt, s_CT = (sem(n) for n in ("s_oh", "s_hist", "s_ji", "s_jf", "s_cnt", "s_CT"))
        s_CTt, s_mk = sem("s_CTt"), sem("s_mk")
        s_xh, s_xl, s_w1h, s_w1l, s_w2h, s_w2l = (sem(n) for n in ("s_xh", "s_xl", "s_w1h", "s_w1l", "s_w2h", "s_w2l"))
        s_B, s_h32, s_hh, s_hl, s_asd = (sem(n) for n in ("s_B", "s_h32", "s_hh", "s_hl", "s_asd"))
        s_lk, s_bc, s_amx, s_zm, s_mc, s_L, s_sub, s_exp = (sem(n) for n in ("s_lk", "s_bc", "s_amx", "s_zm", "s_mc", "s_L", "s_sub", "s_exp"))
        s_P, s_Ph, s_Pl, s_den, s_rb0, s_rb = (sem(n) for n in ("s_P", "s_Ph", "s_Pl", "s_den", "s_rb0", "s_rb"))
        s_A, s_y, s_ex, s_em, s_g, s_gh, s_gl, s_C = (sem(n) for n in ("s_A", "s_y", "s_ex", "s_em", "s_g", "s_gh", "s_gl", "s_C"))
        s_xb, s_D, s_dn, s_res, s_st, s_mv, s_rs, s_fin = (sem(n) for n in ("s_xb", "s_D", "s_dn", "s_res", "s_st", "s_mv", "s_rs", "s_fin"))

        m_src = put("sp", [], lambda: S.dma_start(si[:, :], src.rearrange("(p j) -> p j", p=128)), s_edge, 16)
        m_dst = put("sp", [], lambda: S.dma_start(di[:, :], dst.rearrange("(p j) -> p j", p=128)), s_edg2, 16)
        m_xT = put("sp", [], lambda: S.dma_start(xTr[:, :, :], xT.rearrange("(t p) n -> p t n", p=128)), s_xT, 16)
        m_b1 = put("sp", [], lambda: S.dma_start(b1s[:, :], b1c), s_b1, 16)

        raw = {"n": 0, "free": [None] * NR}

        def load_raw(rows):
            n = raw["n"] % NR
            raw["n"] += 1
            m = put("sp", [raw["free"][n]], lambda: S.dma_start(Wr[:, n, :], rows), s_wr[n], 16)
            return n, m

        w1_m, w2_m = {}, {}
        B_done, C_done, A_done = {}, {}, {}

        def split_w1(h, k):
            n, m = load_raw(W1[128 * k:128 * k + 128, D * h:D * h + D])
            mh = put("act", [m, B_done.get(h - 1)], lambda: A.copy(W1h[:, k, :], Wr[:, n, :]), s_w1h)
            ml = put("pool", [m, mh, B_done.get(h - 1)],
                     lambda: G.tensor_tensor(W1l[:, k, :], Wr[:, n, :], W1h[:, k, :].bitcast(f32), ALU.subtract), s_w1l)
            raw["free"][n] = ml
            w1_m[h, k] = [mh, ml]

        w2 = {"n": 0, "free": [None] * N2}

        def split_w2(h, k):
            n, m = load_raw(W2[D * h + 128 * k:D * h + 128 * k + 128, :])
            q = w2["n"] % N2
            w2["n"] += 1
            mh = put("act", [m, w2["free"][q]], lambda: A.copy(W2h[:, q, :], Wr[:, n, :]), s_w2h)
            ml = put("pool", [m, mh, w2["free"][q]],
                     lambda: G.tensor_tensor(W2l[:, q, :], Wr[:, n, :], W2h[:, q, :].bitcast(f32), ALU.subtract), s_w2l)
            raw["free"][n] = ml
            w2_m[h, k] = (q, [mh, ml])

        abc_m, as_done = {}, {}

        def load_abc(h):
            abc_m[h] = [
                put("sp", [as_done.get(h - 2)],
                    lambda a=a, i=i: S.dma_start(abc[:, h % 2, i, :], a[h:h + 1, :].broadcast_to([128, D])),
                    s_abc[2 * (h % 2) + i], 16)
                for i, a in enumerate((as1, ad1))]

        m_io = put("pool", [], lambda: G.iota(ioi[:, :], pattern=[[1, N]], base=0, channel_multiplier=0), s_io)
        m_oner = put("pool", [], lambda: G.memset(oner[:, :].bitcast(f32), 1.0), s_cst)
        m_z = put("pool", [], lambda: G.memset(idn[:, :], 0.0), s_cst)
        m_idn = put("pool", [m_z], lambda: G.affine_select(
            out=idn[:, :], in_=idn[:, :], compare_op=ALU.not_equal, fill=1.0, base=0,
            pattern=[[-1, 128]], channel_multiplier=1), s_cst)

        m_iof = put("dve", [m_io], lambda: V.tensor_copy(iof[:, :], ioi[:, :]), s_iof)
        m_df = put("dve", [m_dst], lambda: V.tensor_copy(df[:, :], di[:, :]), s_key)
        put("dve", [m_src], lambda: V.tensor_scalar(t1[:, :], si[:, :], 127, None, ALU.bitwise_and), s_key)
        m_t2 = put("dve", [], lambda: V.tensor_scalar(t2[:, :], si[:, :], 1, 128, ALU.logical_shift_right, ALU.bitwise_and), s_key)
        m_t3 = put("dve", [], lambda: V.tensor_scalar(t3[:, :], si[:, :], 7, 1, ALU.logical_shift_right, ALU.bitwise_and), s_key)
        put("dve", [m_t2], lambda: V.tensor_tensor(uf[:, :], t1[:, :], t2[:, :], ALU.add), s_key)
        m_key = put("dve", [m_t3], lambda: V.tensor_scalar(wf[:, :], t3[:, :], float(FIELD - 1), 1.0, ALU.mult, ALU.add), s_key)

        def split_x(k):
            mh = put("act", [m_xT], lambda: A.copy(xTh[:, k, :], xTr[:, k, :]), s_xh)
            ml = put("pool", [mh, m_xT], lambda: G.tensor_tensor(
                xTl[:, k, :], xTr[:, k, :], xTh[:, k, :].bitcast(f32), ALU.subtract), s_xl)
            return mh, ml

        load_abc(0)
        x_m = []
        for k in range(FT):
            x_m.append(split_x(k))
            split_w1(0, k)

        hist = {}
        j = 0
        m_ji, m_jf, m_cnt, m_grp = {}, {}, {}, {}

        def decode(g):
            for b in range(2):
                m_ji[g] = put("act", [m_grp[g], m_jf.get(g - 2)],
                              lambda b=b: A.copy(ji[:, g % 2, b, :], O[2 * (g % 2) + b][:, :]), s_ji)
            to = cnt if g == 0 else jf
            m_jf[g] = None
            put("dve", [m_ji[g], m_cnt.get(g - 1)], lambda: V.tensor_scalar(
                to[:, 0, :, :], ji[:, g % 2, :, :], FIELD - 1, None, ALU.bitwise_and), s_jf)
            m_jf[g] = put("dve", [], lambda: V.tensor_scalar(
                to[:, 1, :, :], ji[:, g % 2, :, :], 12, None, ALU.logical_shift_right), s_jf)
            if g:
                m_cnt[g] = put("pool", [m_jf[g], m_jf[0], m_cnt.get(g - 1)], lambda: G.tensor_tensor(
                    cnt[:, :, :, :], cnt[:, :, :, :], jf[:, :, :, :], ALU.add), s_cnt)

        for g, size in enumerate(GROUPS):
            for b in range(size):
                r = j % OHR
                put("dve", [m_iof, m_df, hist.get(j - OHR)], lambda r=r, j=j: V.tensor_scalar(
                    ohd[:, r, :], iof[:, :], df[:, j:j + 1], None, ALU.is_equal), s_oh)
                m_oh = put("dve", [m_key], lambda r=r, j=j: V.tensor_scalar(
                    ohs[:, r, :], iof[:, 0:256], uf[:, j:j + 1], wf[:, j:j + 1], ALU.is_equal, ALU.mult), s_oh)
                for q in range(2):
                    hist[j] = put("pe", [m_oh, m_ji.get(g - 2)], lambda r=r, q=q, g=g, b=b, size=size: T.matmul(
                        O[2 * (g % 2) + q][:, :], ohs[:, r, 128 * q:128 * q + 128], ohd[:, r, :],
                        start=(b == 0), stop=(b == size - 1)), s_hist)
                j += 1
                if b == 8 and g:
                    decode(g - 1)
            m_grp[g] = hist[j - 1]

        hl_m, hh_m, h32_free, asd_m, P_m, rb_m = {}, {}, [None, None], {}, {}, {}
        pl_m, gh_m, gl_m, y_free, ex_free = {}, {}, {}, [None, None], [None, None]

        def split_h(h, t, slot, get, a_ap, m_a):
            mhh = put("act", slot + [A_done.get(h - 1)], lambda: A.copy(hh[:, t, :], get), s_hh)
            par = h % 2
            for i in range(2):
                m = put("dve", slot + [m_a[i], A_done.get(h - 1) if i == 0 else as_done.get("junk")], lambda i=i: V.tensor_tensor_reduce(
                    out=(hl[:, t, :], junk[:, :])[i], in0=get, in1=a_ap[:, i, :], op0=ALU.mult, op1=ALU.add, scale=1.0, scalar=0.0,
                    accum_out=asd[:, par, i, t:t + 1]), s_asd)
            asd_m[h] = m
            as_done[h] = as_done["junk"] = m
            mhl = put("dve", [mhh, m, A_done.get(h - 1)], lambda: V.tensor_tensor(
                hl[:, t, :], get, hh[:, t, :].bitcast(f32), ALU.subtract), s_hl)
            hh_m[h, t], hl_m[h, t] = mhh, mhl
            return mhl

        def stage_B(h, t):
            ev = []
            for c in range(2):
                k, bk, rel = bank()
                for f in range(FT):
                    passes = ((xTh, W1h), (xTh, W1l), (xTl, W1h))
                    for p, (xa, wa) in enumerate(passes):
                        m = put("pe", [rel, *x_m[f], *w1_m[h, f]], lambda bk=bk, c=c, xa=xa, wa=wa, f=f, p=p: T.matmul(
                            bk[:, 0:HALF], xa[:, f, 128 * t:128 * t + 128], wa[:, f, HALF * c:HALF * c + HALF],
                            start=(f == 0 and p == 0), stop=(f == FT - 1 and p == 2)),
                            s_B if (f == FT - 1 and p == 2) else None)
                B_done[h] = m
                e = put("act", [m, h32_free[t % 2]], lambda bk=bk, c=c: A.copy(
                    h32[:, t % 2, HALF * c:HALF * c + HALF], bk[:, 0:HALF]), s_h32)
                ring["rel"][k] = e
                ev.append(e)
            h32_free[t % 2] = split_h(h, t, [e], h32[:, t % 2, :], abc[:, h % 2, :, :], abc_m[h])

        def bcast(col, m):
            k, bk, rel = bank()
            for t in range(NT):
                mk = put("pe", [rel, m, m_idn], lambda t=t: T.transpose(
                    bk[:, 128 * t:128 * t + 128], col[:, t:t + 1].broadcast_to([128, 128]), idn[:, :]),
                    s_bc if t == NT - 1 else None)
            return k, bk, mk

        def scores_1(h):
            par = h % 2
            ks, bs, ms = bcast(asd[:, par, 0, :], asd_m[h])
            kd, bd, md = bcast(asd[:, par, 1, :], asd_m[h])
            for t in range(NT):
                m = put("dve", [ms, m_mk, A_done.get(h - 1)], lambda t=t: V.tensor_tensor_reduce(
                    out=Pl[:, t, :], in0=bs[:, :], in1=Mk[:, t, :], op0=ALU.add, op1=ALU.max, scale=1.0, scalar=-3e38,
                    accum_out=amx[:, t:t + 1]), s_amx)
            ring["rel"][ks] = m
            mz = put("dve", [m], lambda: V.tensor_tensor(zm[:, :], amx[:, :], asd[:, par, 1, :], ALU.add), s_zm)
            mL = []
            for t in range(NT):
                mL.append(put("act", [md, m_CT, pl_m.get(h - 1)], lambda t=t: A.activation(
                    L[:, t, :], bd[:, :], ACT.Identity, bias=asd[:, par, 0, t:t + 1], scale=1.0), s_L))
            ring["rel"][kd] = mL[-1]
            mm = put("dve", [mz], lambda: V.scalar_tensor_tensor(
                out=mc[:, :], in0=zm[:, :], scalar=SLOPE, in1=zm[:, :], op0=ALU.mult, op1=ALU.max), s_mc)
            for t in range(NT):
                mL[t] = put("dve", [mL[t]], lambda t=t: V.scalar_tensor_tensor(
                    out=L[:, t, :], in0=L[:, t, :], scalar=SLOPE, in1=L[:, t, :], op0=ALU.mult, op1=ALU.max), s_lk)
            P_m[h] = (mL, mm)

        def scores_2(h):
            mL, mm = P_m[h]
            km, bm, m_m = bcast(mc, mm)
            exps = []
            for t in range(NT):
                ms = put("dve", [mL[t], m_m], lambda t=t: V.tensor_tensor(L[:, t, :], L[:, t, :], bm[:, :], ALU.subtract), s_sub)
                exps.append(put("act", [ms], lambda t=t: A.activation(L[:, t, :], L[:, t, :], ACT.Exp), s_exp))
            ring["rel"][km] = ms
            P_m[h] = []
            for t in range(NT):
                mp = put("dve", [exps[t]], lambda t=t: V.scalar_tensor_tensor(
                    out=L[:, t, :], in0=L[:, t, :], scalar=1.0, in1=CT[:, t, :], op0=ALU.min, op1=ALU.mult), s_P)
                mh = put("act", [mp, A_done.get(h - 1)], lambda t=t: A.copy(Ph[:, t, :], L[:, t, :]), s_Ph)
                pl_m[h] = put("pool", [mp, mh, A_done.get(h - 1)], lambda t=t: G.tensor_tensor(
                    Pl[:, t, :], L[:, t, :], Ph[:, t, :].bitcast(f32), ALU.subtract), s_Pl)
                P_m[h].append((mh, pl_m[h]))

        def denom(h):
            k, bk, rel = bank()
            for t in range(NT):
                for i, p in enumerate((Ph, Pl)):
                    m = put("pe", [rel, P_m[h][t][i], m_oner], lambda t=t, i=i, p=p: T.matmul(
                        bk[:, :], oner[:, :], p[:, t, :], start=(t == 0 and i == 0), stop=(t == NT - 1 and i == 1)),
                        s_den if (t == NT - 1 and i == 1) else None)
            m0 = put("dve", [m], lambda: V.tensor_scalar(rb[:, :], bk[:, :], EPS, None, ALU.add), s_rb0)
            ring["rel"][k] = m0
            rb_m[h] = put("dve", [m0], lambda: V.reciprocal(rb[:, :], rb[:, :]), s_rb)

        y_m = {}

        def stage_A(h, c):
            k, bk, rel = bank()
            for t in range(NT):
                passes = ((hh, Ph, [hh_m[h, t], P_m[h][t][0]]), (hh, Pl, [P_m[h][t][1]]), (hl, Ph, [hl_m[h, t]]))
                for p, (ha, pa, ws) in enumerate(passes):
                    m = put("pe", [rel, *ws], lambda ha=ha, pa=pa, t=t, p=p: T.matmul(
                        bk[:, :], ha[:, t, 128 * c:128 * c + 128], pa[:, t, :],
                        start=(t == 0 and p == 0), stop=(t == NT - 1 and p == 2)),
                        s_A if (t == NT - 1 and p == 2) else None)
            A_done[h] = m
            i = c % 2
            my = put("dve", [m, rb_m[h], y_free[i]], lambda: V.tensor_tensor(y[:, i, :], bk[:, :], rb[:, :], ALU.mult), s_y)
            ring["rel"][k] = my
            col = h * FT + c
            y_m[h, c] = put("act", [my, m_b1, ex_free[i]], lambda: A.activation(
                ex[:, i, :], y[:, i, :], ACT.Exp, bias=b1s[:, col:col + 1], scale=1.0), s_ex)

        def elu(h, c):
            i = c % 2
            col = h * FT + c
            me = put("dve", [y_m[h, c]], lambda: V.tensor_scalar(ex[:, i, :], ex[:, i, :], 1.0, 1.0, ALU.min, ALU.subtract), s_em)
            mg = put("dve", [me, m_b1], lambda: V.scalar_tensor_tensor(
                out=y[:, i, :], in0=y[:, i, :], scalar=b1s[:, col:col + 1], in1=ex[:, i, :], op0=ALU.add, op1=ALU.max), s_g)
            ex_free[i] = mg
            gh_m[h, c] = put("act", [mg, C_done.get((h - 1, c))], lambda: A.copy(gh[:, c, :], y[:, i, :]), s_gh)
            gl_m[h, c] = put("pool", [mg, gh_m[h, c], C_done.get((h - 1, c))], lambda: G.tensor_tensor(
                gl[:, c, :], y[:, i, :], gh[:, c, :].bitcast(f32), ALU.subtract), s_gl)
            y_free[i] = gl_m[h, c]

        def stage_C(h, c):
            q, ws = w2_m[h, c]
            for p, (ga, wa) in enumerate(((gh, W2h), (gh, W2l), (gl, W2h))):
                for t in range(NT):
                    for i, (ob, lo, hi) in enumerate(Ocols(t)):
                        first, last = (h == 0 and c == 0 and p == 0), (h == H - 1 and c == FT - 1 and p == 2)
                        end = p == 2 and t == NT - 1 and i == 1
                        m = put("pe", [*ws, gh_m[h, c], gl_m[h, c] if p == 2 else None, m_mk],
                                lambda ga=ga, wa=wa, t=t, ob=ob, lo=lo, hi=hi, i=i, first=first, last=last: T.matmul(
                                    ob, ga[:, c, 128 * t:128 * t + 128], wa[:, q, lo:hi],
                                    start=first and (i == 0 or t % 2 == 0), stop=last, skip_group_check=True),
                                s_C if end else None)
            C_done[h, c] = m
            w2["free"][q] = m

        for h in range(H + 1):
            if h < H:
                if h + 1 < H:
                    load_abc(h + 1)
                for t in range(NT):
                    stage_B(h, t)
                    if h and t < N2:
                        split_w2(h - 1, t)
                    if h == 0 and t == 0:
                        decode(len(GROUPS) - 1)
                        cv = CT[:, :, :].rearrange("p (b f) n -> p f b n", f=2)
                        put("dve", [m_cnt[len(GROUPS) - 1]], lambda: V.tensor_copy(cv[:, 0, :, :], cnt[:, 0, :, :]), s_CT)
                        m_CT = put("dve", [], lambda: V.tensor_copy(cv[:, 1, :, :], cnt[:, 1, :, :]), s_CT)
                    if h == 0 and t == 2:
                        for d in range(NT):
                            for s in range(NT):
                                m = put("pe", [m_CT, m_idn, m_ji[len(GROUPS) - 1]], lambda d=d, s=s: T.transpose(
                                    O[d][:, 128 * s:128 * s + 128], CT[:, s, 128 * d:128 * d + 128], idn[:, :]),
                                    s_CTt if s == NT - 1 else None)
                            m_mk = put("dve", [m], lambda d=d: V.tensor_scalar(
                                Mk[:, d, :], O[d][:, :], 0.0, -BIG, ALU.is_equal, ALU.mult), s_mk)
            if h < H and h == 0:
                scores_1(0)
                scores_2(0)
                for k in range(FT):
                    split_w1(1, k)
                denom(0)
            if h:
                for c in range(FT):
                    stage_C(h - 1, c)
                    if h < H:
                        if c == 0:
                            scores_1(h)
                        if c == 1:
                            scores_2(h)
                        if h + 1 < H and c >= 3:
                            split_w1(h + 1, c - 3)
                    if c + N2 < FT:
                        split_w2(h - 1, c + N2)
                if h < H:
                    denom(h)
            if h < H:
                for c in range(FT):
                    stage_A(h, c)
                    if c:
                        elu(h, c - 1)
                    if h and h + 1 < H and c >= 2 and c - 2 < 3:
                        split_w1(h + 1, c + 1)
                elu(h, FT - 1)
                if h == H - 1:
                    for t in range(N2):
                        split_w2(h, t)

        b7 = B_done[H - 1]
        m_xr = put("sp", [b7], lambda: S.dma_start(xr[:, :, :], x.rearrange("(t p) f -> p t f", p=128)), s_xr, 16)
        m_b2 = put("sp", [b7], lambda: S.dma_start(b2b[:, :], b2.unsqueeze(0).broadcast_to([128, D])), s_b2, 16)
        m_a2 = [put("sp", [b7], lambda i=i, a=a: S.dma_start(a2b[:, i, :], a[0:1, :].broadcast_to([128, D])), s_a2[i], 16)
                for i, a in enumerate((as2, ad2))]
        for t in range(NT):
            m_xb = put("dve", [m_xr, m_b2], lambda t=t: V.tensor_tensor(xr[:, t, :], xr[:, t, :], b2b[:, :], ALU.add), s_xb)
        hdone = C_done[H - 1, FT - 1]
        evs = []
        for t in range(NT):
            for ob, lo, hi in Ocols(t):
                e = put("act", [hdone, b7], lambda t=t, ob=ob, lo=lo, hi=hi: A.copy(res[:, t, lo:hi], ob), s_h32)
            evs.append(e)
            split_h(H, t, [e], res[:, t, :], a2b, m_a2)
        scores_1(H)
        scores_2(H)
        kd, bd, rel = bank()
        for t in range(NT):
            for i, p in enumerate((Ph, Pl)):
                for d in range(NT):
                    m = put("pe", [rel, P_m[H][t][i]], lambda t=t, i=i, p=p, d=d: T.matmul(
                        bd[:, 2 * d:2 * d + 2], p[:, t, 128 * d:128 * d + 128], oner[:, 0:2],
                        start=(t == 0 and i == 0 and d == 0), stop=(t == NT - 1 and i == 1), skip_group_check=True),
                        s_den if (t == NT - 1 and i == 1 and d == NT - 1) else None)
        dnf = dn[:, :, :].rearrange("p t c -> p (t c)")
        m0 = put("dve", [m], lambda: V.tensor_scalar(dnf, bd[:, 0:2 * NT], EPS, None, ALU.add), s_dn)
        m_dn = put("dve", [m0], lambda: V.reciprocal(dnf, dnf), s_dn)
        outv = out.rearrange("(t p) f -> p t f", p=128)
        mr_m = {}
        for d in range(NT):
            pieces = [(O[d][:, 0:512], 0, 512), (O[4 + d % 2][:, 0:256], 512, 768)]
            for t in range(NT):
                for p, (pa, ha, ws) in enumerate(((Ph, hh, [hh_m[H, t]]), (Pl, hh, []), (Ph, hl, [hl_m[H, t]]))):
                    for i, (ob, lo, hi) in enumerate(pieces):
                        end = t == NT - 1 and p == 2
                        m = put("pe", [evs[-1], mr_m.get(d - 2), *ws], lambda d=d, t=t, p=p, pa=pa, ha=ha, ob=ob, lo=lo, hi=hi, i=i, end=end: T.matmul(
                            ob, pa[:, t, 128 * d:128 * d + 128], ha[:, t, lo:hi],
                            start=(t == 0 and p == 0), stop=end),
                            s_D if end and i == 1 else None)
            for i, (ob, lo, hi) in enumerate(pieces):
                mr = put("dve", [m, m_dn, m_xb, hl_m[H, d]], lambda d=d, ob=ob, lo=lo, hi=hi: V.scalar_tensor_tensor(
                    out=res[:, d, lo:hi], in0=ob, scalar=dn[:, d, 0:1], in1=xr[:, d, lo:hi], op0=ALU.mult, op1=ALU.add), s_res)
            mr_m[d] = mr
            for i in range(2):
                ms = put("dve", [mr], lambda d=d, i=i: V.bn_stats(st6[:, d, i, :], res[:, d, HALF * i:HALF * i + HALF]), s_st)
            mm = put("dve", [ms], lambda d=d: V.bn_aggr(mv[:, d, :], st6[:, d, :, :]), s_mv)
            mv1 = put("dve", [mm], lambda d=d: V.tensor_scalar(rs[:, d, 1:2], mv[:, d, 1:2], LN_EPS, None, ALU.add), s_mv)
            m1 = put("act", [mv1], lambda d=d: A.activation(rs[:, d, 0:1], rs[:, d, 1:2], ACT.Sqrt), s_rs)
            m2 = put("dve", [m1], lambda d=d: V.reciprocal(rs[:, d, 1:2], rs[:, d, 0:1]), s_mv)
            mf = put("dve", [m2], lambda d=d: V.tensor_scalar(
                res[:, d, :], res[:, d, :], mv[:, d, 0:1], rs[:, d, 1:2], ALU.subtract, ALU.mult), s_fin)
            last = put("sp", [mf], lambda d=d: S.dma_start(outv[:, d, :], res[:, d, :]), s_out, 16)
        queue["sp"].append(lambda e: e.wait_ge(last[0][1], last[1]))

        with nc.Block() as block:
            def run(name):
                def body(e):
                    for step in queue[name]:
                        step(e)
                return body
            block.sync(run("sp"))
            block.scalar(run("act"))
            block.vector(run("dve"))
            block.gpsimd(run("pool"))
            block.tensor(run("pe"))


def kernel(**inputs):
    import numpy as np
    import concourse.bacc as bacc
    from concourse import mybir as mb
    from concourse.bass_utils import run_bass_kernel_spmd

    nc = bacc.Bacc("TRN2", target_bir_lowering=False, num_devices=1)
    p = "L0_gnn_"
    x = np.asarray(inputs["x"])
    b1 = np.asarray(inputs[p + "b1"])
    given = [("x", x), ("xT", x.T), ("src", inputs["src"]), ("dst", inputs["dst"]), ("W1", inputs[p + "W1"]),
             ("as1", inputs[p + "a_src1"]), ("ad1", inputs[p + "a_dst1"]), ("b1c", b1.reshape(48, 128).T),
             ("W2", inputs[p + "W2"]), ("as2", inputs[p + "a_src2"]), ("ad2", inputs[p + "a_dst2"]),
             ("b2", inputs[p + "b2"])]
    arrays, args = {}, []
    for name, a in given:
        a = np.ascontiguousarray(np.asarray(a))
        arrays[f"in_{name}"] = a
        args.append(nc.dram_tensor(f"in_{name}", a.shape, mb.dt.from_np(a.dtype), kind="ExternalInput").ap())
    o = nc.dram_tensor("out_0", (512, 768), mb.dt.float32, kind="ExternalOutput").ap()
    gat_resnorm_kernel(nc, *args, o)
    r = run_bass_kernel_spmd(nc, [arrays], core_ids=[0])
    return r.results[0]["out_0"]
```

```python
import concourse.bass as bass
from concourse import mybir
from contextlib import ExitStack


def gat_resnorm_kernel(nc, x, xT, src, dst, W1, as1, ad1, b1c, W2, as2, ad2, b2, out):
    f32, f32r, bf16 = mybir.dt.float32, mybir.dt.float32r, mybir.dt.bfloat16
    i32, f16 = mybir.dt.int32, mybir.dt.float16
    ALU, ACT = mybir.AluOpType, mybir.ActivationFunctionType

    N, D, H, E = 512, 768, 8, 16896
    NT, FT = N // 128, D // 128
    HALF = D // 2
    EJ = E // 128
    GROUPS = [27, 27, 26, 26, 26]
    OHR = 8
    FIELD = 4096
    SLOPE, EPS, LN_EPS, BIG = 0.2, 1e-16, 1e-5, 1e30
    NR, N2, NY, LASTC = 5, 4, 3, 3

    queue = {"sp": [], "act": [], "dve": [], "pool": [], "pe": []}
    count, seen = {}, {}
    ctx = ExitStack()
    with ctx:
        def sem(name):
            s = ctx.enter_context(nc.semaphore(name))
            count[name] = 0
            return (name, s)

        def put(eng, waits, fn, done=None, by=1):
            for w in waits:
                if w is None:
                    continue
                (name, s), v = w
                if seen.get((eng, name), 0) < v:
                    seen[eng, name] = v
                    queue[eng].append(lambda e, s=s, v=v: e.wait_ge(s, v))
            if done is None:
                queue[eng].append(lambda e: fn())
                return None
            count[done[0]] += by
            queue[eng].append(lambda e: fn().then_inc(done[1], by))
            return (done, count[done[0]])

        def sb(name, shape, dt, where=ctx):
            return where.enter_context(nc.sbuf_tensor(name, shape, dt))

        V, A, G, T, S = nc.vector, nc.scalar, nc.gpsimd, nc.tensor, nc.sync

        xTh = sb("xTh", [128, FT, N], f32r)
        xTl = sb("xTl", [128, FT, N], f32r)
        CT = sb("CT", [128, NT, N], f32)
        Mk = sb("Mk", [128, NT, N], bf16)
        Wr = sb("Wr", [128, NR, D], f32)
        W2h = sb("W2h", [128, N2, D], f32r)
        W2l = sb("W2l", [128, N2, D], f32r)
        h32 = sb("h32", [128, 2, D], f32)
        hh = sb("hh", [128, NT, D], f32r)
        hl = sb("hl", [128, NT, D], f32r)
        abc = sb("abc", [128, 2, 2, D], f32)
        rb = sb("rb", [128, N], f32)
        idn = sb("idn", [128, 128], f32)
        oner = sb("oner", [128, 128], f32r)
        b1s = sb("b1s", [128, H * FT], f32)
        asd = sb("asd", [128, 2, 2, NT], f32)
        amx = sb("amx", [128, NT], f32)
        zm = sb("zm", [128, NT], f32)
        mc = sb("mc", [128, NT], f32)
        junk = sb("junk", [128, D], bf16)
        with ExitStack() as c1:
            W1h = sb("W1h", [128, FT, D], f32r, c1)
            W1l = sb("W1l", [128, FT, D], f32r, c1)
        c2 = ctx.enter_context(ExitStack())
        xr = sb("xr", [128, NT, D], f32, c2)
        res = sb("res", [128, NT, D], f32, c2)
        b2b = sb("b2b", [128, D], f32, c2)
        a2b = sb("a2b", [128, 2, D], f32, c2)
        st6 = sb("st6", [128, NT, 2, 6], f32, c2)
        mv = sb("mv", [128, NT, 2], f32, c2)
        rs = sb("rs", [128, NT, 2], f32, c2)
        dn = sb("dn", [128, NT, 2], f32, c2)
        sb("pad", [128, 9216 - (2 * NT * D + 3 * D + NT * 12 + 3 * NT * 2)], f32, c2)
        with ExitStack() as c3:
            si = sb("si", [128, EJ], i32, c3)
            di = sb("di", [128, EJ], i32, c3)
            t1 = sb("t1", [128, EJ], i32, c3)
            t2 = sb("t2", [128, EJ], i32, c3)
            t3 = sb("t3", [128, EJ], i32, c3)
            df = sb("df", [128, EJ], f32, c3)
            uf = sb("uf", [128, EJ], f32, c3)
            wf = sb("wf", [128, EJ], f32, c3)
            nuf = sb("nuf", [128, EJ], f32, c3)
            nwf = sb("nwf", [128, EJ], f32, c3)
            dist = sb("dist", [128, 2, 256], f16, c3)
            ioi = sb("ioi", [128, N], i32, c3)
            iof = sb("iof", [128, N], f16, c3)
            ohd = sb("ohd", [128, OHR, N], bf16, c3)
            ohs = sb("ohs", [128, OHR, 256], bf16, c3)
            ji = sb("ji", [128, 2, 2, N], i32, c3)
            jf = sb("jf", [128, 2, 2, N], i32, c3)
            cnt = sb("cnt", [128, 2, 2, N], i32, c3)
        L = sb("L", [128, NT, N], f32)
        Ph = sb("Ph", [128, NT, N], f32r)
        Pl = sb("Pl", [128, NT, N], f32r)
        y2 = sb("y2", [128, N], f32)
        gh = sb("gh", [128, FT, N], f32r)
        gl = sb("gl", [128, FT, N], f32r)

        ys = [L[:, 0, :], L[:, 1, :], y2[:, :]]
        exs = [L[:, 2, :], L[:, 3, :]]

        O = [ctx.enter_context(nc.psum_tensor(f"O{i}", [128, 512], f32)) for i in range(6)]
        R = [ctx.enter_context(nc.psum_tensor(f"R{i}", [128, 512], f32)) for i in range(2)]

        def Ocols(t):
            return [(O[t][:, 0:512], 0, 512), (O[4 + t // 2][:, 256 * (t % 2):256 * (t % 2) + 256], 512, 768)]

        ring = {"k": 0, "rel": [None, None]}

        def bank():
            k = ring["k"] % 2
            ring["k"] += 1
            return k, R[k], ring["rel"][k]

        s_edge, s_b1, s_out = sem("s_edge"), sem("s_b1"), sem("s_out")
        s_edg2 = sem("s_edg2")
        s_wr = [sem(f"s_wr{i}") for i in range(NR)]
        s_abc = [sem(f"s_abc{i}") for i in range(4)]
        s_xr, s_b2, s_a2 = sem("s_xr"), sem("s_b2"), [sem("s_a20"), sem("s_a21")]
        s_io, s_cst, s_iof, s_key = sem("s_io"), sem("s_cst"), sem("s_iof"), sem("s_key")
        s_ds, s_os, s_oh, s_hist, s_ji, s_jf, s_cnt, s_CT = (sem(n) for n in ("s_ds", "s_os", "s_oh", "s_hist", "s_ji", "s_jf", "s_cnt", "s_CT"))
        s_CTt, s_mk = sem("s_CTt"), sem("s_mk")
        s_w1d, s_xh, s_xl, s_w1h, s_w1l, s_w2h, s_w2l = (sem(n) for n in ("s_w1d", "s_xh", "s_xl", "s_w1h", "s_w1l", "s_w2h", "s_w2l"))
        s_B, s_h32, s_hh, s_hl, s_asd = (sem(n) for n in ("s_B", "s_h32", "s_hh", "s_hl", "s_asd"))
        s_Pd, s_sd, s_sm, s_lk, s_bc, s_amx, s_zm, s_mc, s_L, s_sub, s_exp = (sem(n) for n in ("s_Pd", "s_sd", "s_sm", "s_lk", "s_bc", "s_amx", "s_zm", "s_mc", "s_L", "s_sub", "s_exp"))
        s_P, s_Ph, s_Pl, s_den, s_rb0, s_rb = (sem(n) for n in ("s_P", "s_Ph", "s_Pl", "s_den", "s_rb0", "s_rb"))
        s_A, s_y, s_ex, s_em, s_g, s_gh, s_gl, s_C = (sem(n) for n in ("s_A", "s_y", "s_ex", "s_em", "s_g", "s_gh", "s_gl", "s_C"))
        s_xb, s_D, s_dn, s_res, s_st, s_mv, s_rs, s_fin = (sem(n) for n in ("s_xb", "s_D", "s_dn", "s_res", "s_st", "s_mv", "s_rs", "s_fin"))

        m_src = put("sp", [], lambda: S.dma_start(si[:, :], src.rearrange("(p j) -> p j", p=128)), s_edge, 16)
        m_dst = put("sp", [], lambda: S.dma_start(di[:, :], dst.rearrange("(p j) -> p j", p=128)), s_edg2, 16)
        m_b1 = put("sp", [], lambda: S.dma_start(b1s[:, :], b1c), s_b1, 16)

        raw = {"n": 0, "free": [None] * NR}

        def load_raw(rows, width=D):
            n = raw["n"] % NR
            raw["n"] += 1
            m = put("sp", [raw["free"][n]], lambda: S.dma_start(Wr[:, n, 0:width], rows), s_wr[n], 16)
            return n, m

        w1_m, w2_m = {}, {}
        B_done, C_done, A_done = {}, {}, {}

        def split_w1(h, k, low="pool"):
            n, m = load_raw(W1[128 * k:128 * k + 128, D * h:D * h + D])
            mh = put("act", [m, B_done.get(h - 1)], lambda: A.copy(W1h[:, k, :], Wr[:, n, :]), s_w1h)
            eng = G if low == "pool" else V
            ml = put(low, [m, mh, B_done.get(h - 1)],
                     lambda: eng.tensor_tensor(W1l[:, k, :], Wr[:, n, :], W1h[:, k, :].bitcast(f32), ALU.subtract), s_w1l if low == "pool" else s_w1d)
            raw["free"][n] = ml
            w1_m[h, k] = [mh, ml]

        w2 = {"n": 0, "free": [None] * N2}

        def split_w2(h, k):
            n, m = load_raw(W2[D * h + 128 * k:D * h + 128 * k + 128, :])
            q = w2["n"] % N2
            w2["n"] += 1
            mh = put("act", [m, w2["free"][q]], lambda: A.copy(W2h[:, q, :], Wr[:, n, :]), s_w2h)
            ml = put("pool", [m, mh, w2["free"][q]],
                     lambda: G.tensor_tensor(W2l[:, q, :], Wr[:, n, :], W2h[:, q, :].bitcast(f32), ALU.subtract), s_w2l)
            raw["free"][n] = ml
            w2_m[h, k] = (q, [mh, ml])

        abc_m, as_done = {}, {}

        def load_abc(h):
            abc_m[h] = [
                put("sp", [as_done.get(h - 2)],
                    lambda a=a, i=i: S.dma_start(abc[:, h % 2, i, :], a[h:h + 1, :].broadcast_to([128, D])),
                    s_abc[2 * (h % 2) + i], 16)
                for i, a in enumerate((as1, ad1))]

        m_io = put("pool", [], lambda: G.iota(ioi[:, :], pattern=[[1, N]], base=0, channel_multiplier=0), s_io)
        m_oner = put("pool", [], lambda: G.memset(oner[:, :].bitcast(f32), 1.0), s_cst)
        m_z = put("pool", [], lambda: G.memset(idn[:, :], 0.0), s_cst)
        m_idn = put("pool", [m_z], lambda: G.affine_select(
            out=idn[:, :], in_=idn[:, :], compare_op=ALU.not_equal, fill=1.0, base=0,
            pattern=[[-1, 128]], channel_multiplier=1), s_cst)

        m_iof = put("dve", [m_io], lambda: V.tensor_copy(iof[:, :], ioi[:, :]), s_iof)
        m_df = put("dve", [m_dst], lambda: V.tensor_copy(df[:, :], di[:, :]), s_key)
        put("dve", [m_src], lambda: V.tensor_scalar(t1[:, :], si[:, :], 127, None, ALU.bitwise_and), s_key)
        m_t2 = put("dve", [], lambda: V.tensor_scalar(t2[:, :], si[:, :], 1, 128, ALU.logical_shift_right, ALU.bitwise_and), s_key)
        m_t3 = put("dve", [], lambda: V.tensor_scalar(t3[:, :], si[:, :], 7, 1, ALU.logical_shift_right, ALU.bitwise_and), s_key)
        put("dve", [m_t2], lambda: V.tensor_tensor(uf[:, :], t1[:, :], t2[:, :], ALU.add), s_key)
        m_key = put("dve", [m_t3], lambda: V.tensor_scalar(wf[:, :], t3[:, :], float(FIELD - 1), 1.0, ALU.mult, ALU.add), s_key)

        m_nu = put("dve", [m_key], lambda: V.tensor_scalar(nuf[:, :], uf[:, :], -1.0, None, ALU.mult), s_key)
        m_nw = put("dve", [m_key], lambda: V.tensor_scalar(nwf[:, :], wf[:, :], -1.0, None, ALU.mult), s_key)

        def split_x(k):
            n, m = load_raw(xT[128 * k:128 * k + 128, :], N)
            mh = put("act", [m], lambda: A.copy(xTh[:, k, :], Wr[:, n, 0:N]), s_xh)
            ml = raw["free"][n] = put("pool", [mh, m], lambda: G.tensor_tensor(
                xTl[:, k, :], Wr[:, n, 0:N], xTh[:, k, :].bitcast(f32), ALU.subtract), s_xl)
            return mh, ml

        load_abc(0)
        x_m = []

        hist = {}
        j, m_act = 0, [None, None]
        m_ji, m_jf, m_cnt, m_grp = {}, {}, {}, {}

        def decode(g):
            for b in range(2):
                m_ji[g] = put("act", [m_grp[g], m_jf.get(g - 2)],
                              lambda b=b: A.copy(ji[:, g % 2, b, :], O[2 * (g % 2) + b][:, :]), s_ji)
            to = cnt if g == 0 else jf
            m_jf[g] = None
            put("dve", [m_ji[g], m_cnt.get(g - 1)], lambda: V.tensor_scalar(
                to[:, 0, :, :], ji[:, g % 2, :, :], FIELD - 1, None, ALU.bitwise_and), s_jf)
            m_jf[g] = put("dve", [], lambda: V.tensor_scalar(
                to[:, 1, :, :], ji[:, g % 2, :, :], 12, None, ALU.logical_shift_right), s_jf)
            if 0 < g < len(GROUPS) - 1:
                m_cnt[g] = put("pool", [m_jf[g], m_jf[0], m_cnt.get(g - 1)], lambda: G.tensor_tensor(
                    cnt[:, :, :, :], cnt[:, :, :, :], jf[:, :, :, :], ALU.add), s_cnt)

        for g, size in enumerate(GROUPS):
            for b in range(size):
                r = j % OHR
                m_oh = put("dve", [m_iof, m_df, hist.get(j - OHR)], lambda r=r, j=j: V.tensor_scalar(
                    ohd[:, r, :], iof[:, :], df[:, j:j + 1], None, ALU.is_equal), s_oh)
                if j % 3 == 2:
                    z = (j // 3) % 2
                    m_ds = put("act", [m_iof, m_nw, m_act[z]], lambda z=z, j=j: A.activation(
                        dist[:, z, :], iof[:, 0:256], ACT.Abs, bias=nuf[:, j:j + 1], scale=1.0), s_ds)
                    m_os = m_act[z] = put("act", [m_ds, hist.get(j - OHR)], lambda z=z, r=r, j=j: A.activation(
                        ohs[:, r, :], dist[:, z, :], ACT.Relu, bias=wf[:, j:j + 1], scale=nwf[:, j:j + 1]), s_os)
                else:
                    m_os = put("dve", [m_key], lambda r=r, j=j: V.tensor_scalar(
                        ohs[:, r, :], iof[:, 0:256], uf[:, j:j + 1], wf[:, j:j + 1], ALU.is_equal, ALU.mult), s_oh)
                for q in range(2):
                    hist[j] = put("pe", [m_oh, m_os, m_ji.get(g - 2)], lambda r=r, q=q, g=g, b=b, size=size: T.matmul(
                        O[2 * (g % 2) + q][:, :], ohs[:, r, 128 * q:128 * q + 128], ohd[:, r, :],
                        start=(b == 0), stop=(b == size - 1)), s_hist)
                j += 1
                if j % 8 == 0 and j // 8 <= FT:
                    x_m.append(split_x(j // 8 - 1))
                if j % 8 == 4 and 12 <= j < 12 + 8 * FT:
                    split_w1(0, j // 8 - 1)
                if b == 8 and g:
                    decode(g - 1)
            m_grp[g] = hist[j - 1]

        sm_m, L_free = {}, [None, None]
        hl_m, hh_m, h32_free, asd_m, P_m, rb_m = {}, {}, [None, None], {}, {}, {}
        pl_m, gh_m, gl_m, y_free, ex_free = {}, {}, {}, [None] * NY, [None, None]

        def sums_h(h, t, ready, get, a_ap, m_a):
            for i in range(2):
                m = put("dve", [ready, m_a[i], as_done.get("junk")], lambda i=i: V.tensor_tensor_reduce(
                    out=junk[:, :], in0=get, in1=a_ap[:, i, :], op0=ALU.mult, op1=ALU.add, scale=1.0, scalar=0.0,
                    accum_out=asd[:, h % 2, i, t:t + 1]), s_asd)
                as_done["junk"] = m
            asd_m[h] = as_done[h] = m

        def split_h(h, t, ready, get):
            hh_m[h, t] = put("act", [ready, A_done.get(h - 1)], lambda: A.copy(hh[:, t, :], get), s_hh)
            hl_m[h, t] = put("dve", [hh_m[h, t], A_done.get(h - 1)], lambda: V.tensor_tensor(
                hl[:, t, :], get, hh[:, t, :].bitcast(f32), ALU.subtract), s_hl)

        h32_m = {}

        def half_B(h, t, c):
            k, bk, rel = bank()
            for f in range(FT):
                for p, (xa, wa) in enumerate(((xTh, W1h), (xTh, W1l), (xTl, W1h))):
                    end = f == FT - 1 and p == 2
                    m = put("pe", [rel, *x_m[f], w1_m[h, f][0], w1_m[h, f][1] if p else None],
                            lambda xa=xa, wa=wa, f=f, p=p, end=end: T.matmul(
                                bk[:, 0:HALF], xa[:, f, 128 * t:128 * t + 128], wa[:, f, HALF * c:HALF * c + HALF],
                                start=(f == 0 and p == 0), stop=end), s_B if end else None)
            B_done[h] = m
            h32_m[h, t] = ring["rel"][k] = put("act", [m, h32_free[t % 2]], lambda: A.copy(
                h32[:, t % 2, HALF * c:HALF * c + HALF], bk[:, 0:HALF]), s_h32)

        def sums_B(h, t):
            sums_h(h, t, h32_m[h, t], h32[:, t % 2, :], abc[:, h % 2, :, :], abc_m[h])

        def split_B(h, t):
            split_h(h, t, h32_m[h, t], h32[:, t % 2, :])
            h32_free[t % 2] = hl_m[h, t]

        def bcast(col, m):
            k, bk, rel = bank()
            for t in range(NT):
                mk = put("pe", [rel, m, m_idn], lambda t=t: T.transpose(
                    bk[:, 128 * t:128 * t + 128], col[:, t:t + 1].broadcast_to([128, 128]), idn[:, :]),
                    s_bc if t == NT - 1 else None)
            return k, bk, mk

        def scores_1(h):
            par = h % 2
            ks, bs, ms = bcast(asd[:, par, 0, :], asd_m[h])
            kd, bd, md = bcast(asd[:, par, 1, :], asd_m[h])
            for t in range(NT):
                m = put("dve", [ms, m_mk[t], A_done.get(h - 1)], lambda t=t: V.tensor_tensor_reduce(
                    out=Pl[:, t, :], in0=bs[:, :], in1=Mk[:, t, :], op0=ALU.add, op1=ALU.max, scale=1.0, scalar=-3e38,
                    accum_out=amx[:, t:t + 1]), s_amx)
            ring["rel"][ks] = m
            mz = put("dve", [m], lambda: V.tensor_tensor(zm[:, :], amx[:, :], asd[:, par, 1, :], ALU.add), s_zm)
            mL = []
            for t in range(NT):
                mL.append(put("act", [md, m_CT, *L_free], lambda t=t: A.activation(
                    L[:, t, :], bd[:, :], ACT.Identity, bias=asd[:, par, 0, t:t + 1], scale=1.0), s_L))
            ring["rel"][kd] = mL[-1]
            mm = put("dve", [mz], lambda: V.scalar_tensor_tensor(
                out=mc[:, :], in0=zm[:, :], scalar=SLOPE, in1=zm[:, :], op0=ALU.mult, op1=ALU.max), s_mc)
            for t in range(NT):
                mL[t] = put("dve", [mL[t]], lambda t=t: V.scalar_tensor_tensor(
                    out=L[:, t, :], in0=L[:, t, :], scalar=SLOPE, in1=L[:, t, :], op0=ALU.mult, op1=ALU.max), s_lk)
            P_m[h] = (mL, mm)

        def scores_2(h):
            mL, mm = P_m[h]
            km, bm, m_m = bcast(mc, mm)
            exps = []
            for t in range(NT):
                ms = put("dve", [mL[t], m_m], lambda t=t: V.tensor_tensor(L[:, t, :], L[:, t, :], bm[:, :], ALU.subtract), s_sub)
                exps.append(put("act", [ms], lambda t=t: A.activation(L[:, t, :], L[:, t, :], ACT.Exp), s_exp))
            ring["rel"][km] = ms
            P_m[h] = []
            for t in range(NT):
                mp = put("dve", [exps[t]], lambda t=t: V.scalar_tensor_tensor(
                    out=L[:, t, :], in0=L[:, t, :], scalar=1.0, in1=CT[:, t, :], op0=ALU.min, op1=ALU.mult), s_P)
                mh = put("act", [mp, A_done.get(h - 1)], lambda t=t: A.copy(Ph[:, t, :], L[:, t, :]), s_Ph)
                P_m[h].append([mh, mp])
            for t in range(NT):
                low, mine = ("dve", V) if h == H and t % 2 else ("pool", G)
                pl_m[h] = P_m[h][t][1] = put(low, [P_m[h][t][1], P_m[h][t][0], A_done.get(h - 1)], lambda t=t, mine=mine: mine.tensor_tensor(
                    Pl[:, t, :], L[:, t, :], Ph[:, t, :].bitcast(f32), ALU.subtract), s_Pl if mine is G else s_Pd)
            low, mine = ("dve", V) if h == H else ("pool", G)
            sm = None
            for a, b in ((0, 1), (2, 3), (0, 2)):
                sm = put(low, [*P_m[h][a], *P_m[h][b], sm], lambda a=a, b=b: mine.tensor_tensor(
                    L[:, a, :], L[:, a, :], L[:, b, :], ALU.add), s_sm if mine is G else s_sd)
            sm_m[h] = sm

        def denom(h):
            k, bk, rel = bank()
            m = put("pe", [rel, sm_m[h], m_oner], lambda: T.matmul(
                bk[:, :], oner[:, :].bitcast(f32), L[:, 0, :], start=True, stop=True), s_den)
            m0 = put("dve", [m], lambda: V.tensor_scalar(rb[:, :], bk[:, :], EPS, None, ALU.add), s_rb0)
            ring["rel"][k] = m0
            rb_m[h] = put("dve", [m0], lambda: V.reciprocal(rb[:, :], rb[:, :]), s_rb)

        y_m = {}

        def stage_A(h, c):
            k, bk, rel = bank()
            for t in range(NT):
                passes = ((hh, Ph, [hh_m[h, t], P_m[h][t][0]]), (hh, Pl, [P_m[h][t][1]]), (hl, Ph, [hl_m[h, t]]))
                for p, (ha, pa, ws) in enumerate(passes):
                    m = put("pe", [rel, *ws], lambda ha=ha, pa=pa, t=t, p=p: T.matmul(
                        bk[:, :], ha[:, t, 128 * c:128 * c + 128], pa[:, t, :],
                        start=(t == 0 and p == 0), stop=(t == NT - 1 and p == 2)),
                        s_A if (t == NT - 1 and p == 2) else None)
            A_done[h] = m
            my = put("dve", [m, rb_m[h], y_free[c % NY]], lambda: V.tensor_tensor(ys[c % NY], bk[:, :], rb[:, :], ALU.mult), s_y)
            ring["rel"][k] = my
            col = h * FT + c
            y_m[h, c] = put("act", [my, m_b1, ex_free[c % 2]], lambda: A.activation(
                exs[c % 2], ys[c % NY], ACT.Exp, bias=b1s[:, col:col + 1], scale=1.0), s_ex)

        def elu(h, c):
            yt, et = ys[c % NY], exs[c % 2]
            col = h * FT + c
            me = put("dve", [y_m[h, c]], lambda: V.tensor_scalar(et, et, 1.0, 1.0, ALU.min, ALU.subtract), s_em)
            mg = put("dve", [me, m_b1], lambda: V.scalar_tensor_tensor(
                out=yt, in0=yt, scalar=b1s[:, col:col + 1], in1=et, op0=ALU.add, op1=ALU.max), s_g)
            ex_free[c % 2] = L_free[1] = mg
            gh_m[h, c] = put("act", [mg, C_done.get((h - 1, c))], lambda: A.copy(gh[:, c, :], yt), s_gh)

        def elu_low(h, c):
            gl_m[h, c] = put("dve", [gh_m[h, c], C_done.get((h - 1, c))], lambda: V.tensor_tensor(
                gl[:, c, :], ys[c % NY], gh[:, c, :].bitcast(f32), ALU.subtract), s_gl)
            y_free[c % NY] = L_free[0] = gl_m[h, c]

        PIECES = [[p for t in (0, 1) for p in [(t, *Ocols(t)[1])]], [(0, *Ocols(0)[0])], [(1, *Ocols(1)[0])],
                  [p for t in (2, 3) for p in [(t, *Ocols(t)[1])]], [(2, *Ocols(2)[0])], [(3, *Ocols(3)[0])]]
        bank_m = {}

        def stage_C(h, c, only=None):
            q, ws = w2_m[h, c]
            for p, (ga, wa) in enumerate(((gh, W2h), (gh, W2l), (gl, W2h))):
                for n, group in enumerate(PIECES):
                    for t, ob, lo, hi in group:
                        if only not in (None, n):
                            continue
                        first, last = (h == 0 and c == 0 and p == 0), (h == H - 1 and c == FT - 1 and p == 2)
                        m = put("pe", [ws[0], ws[1] if p else None, gh_m[h, c], gl_m[h, c] if p == 2 else None, m_mk[NT - 1]],
                                lambda ga=ga, wa=wa, t=t, ob=ob, lo=lo, hi=hi, first=first, last=last: T.matmul(
                                    ob, ga[:, c, 128 * t:128 * t + 128], wa[:, q, lo:hi],
                                    start=first and (hi - lo == 512 or t % 2 == 0), stop=last, skip_group_check=True),
                                s_C if p == 2 and t == group[-1][0] and n == (5 if only is None else only) else None)
            C_done[h, c] = w2["free"][q] = m
            if only is not None:
                bank_m[only] = m

        def counts_end():
            g = len(GROUPS) - 1
            decode(g)
            cv = CT[:, :, :].rearrange("p (b f) n -> p f b n", f=2)
            for i in range(2):
                m = put("dve", [m_cnt[g - 1], m_jf[g]], lambda i=i: V.tensor_tensor(
                    cv[:, i, :, :], cnt[:, i, :, :], jf[:, i, :, :], ALU.add), s_CT)
            return m

        def masks():
            out_m = []
            for d in range(NT):
                for s in range(NT):
                    m = put("pe", [m_CT, m_idn, m_ji[len(GROUPS) - 1]], lambda d=d, s=s: T.transpose(
                        O[d][:, 128 * s:128 * s + 128], CT[:, s, 128 * d:128 * d + 128], idn[:, :]),
                        s_CTt if s == NT - 1 else None)
                out_m.append(put("dve", [m], lambda d=d: V.tensor_scalar(
                    Mk[:, d, :], O[d][:, :], 0.0, -BIG, ALU.is_equal, ALU.mult), s_mk))
            return out_m

        def mix(h, splits):
            for c in range(FT):
                stage_A(h, c)
                if c > 1:
                    elu_low(h, c - 2)
                if c:
                    elu(h, c - 1)
                if c < len(splits):
                    splits[c][0](*splits[c][1:])
            elu(h, FT - 1)
            elu_low(h, FT - 2)
            elu_low(h, FT - 1)

        load_abc(1)
        for t in range(NT):
            for c in range(2):
                half_B(0, t, c)
            sums_B(0, t)
            split_B(0, t)
            if t == 0:
                m_CT = counts_end()
            if t == 2:
                m_mk = masks()
        scores_1(0)
        for k in range(FT):
            split_w1(1, k, "dve" if k % 2 else "pool")
        half_B(1, 0, 0)
        scores_2(0)
        half_B(1, 0, 1)
        sums_B(1, 0)
        half_B(1, 1, 0)
        half_B(1, 1, 1)
        denom(0)
        sums_B(1, 1)
        mix(0, [(split_w2, 0, t) for t in range(N2)])
        for h in range(1, H):
            if h + 1 < H:
                load_abc(h + 1)
            for t in range(NT):
                if h > 1 or t > 1:
                    for c in range(2):
                        half_B(h, t, c)
                    sums_B(h, t)
                split_B(h, t)
                if h > 1:
                    split_w2(h - 1, t)
            stage_C(h - 1, 0)
            scores_1(h)
            split_w2(h - 1, 4)
            stage_C(h - 1, 1)
            split_w2(h - 1, 5)
            scores_2(h)
            for c in range(2, FT):
                stage_C(h - 1, c)
                if h + 1 < H:
                    split_w1(h + 1, c - 2)
            denom(h)
            if h + 1 < H:
                mix(h, [(split_w1, h + 1, 4), (split_w1, h + 1, 5)])
            else:
                mix(h, [(split_w2, h, t) for t in range(N2)])

        b7 = B_done[H - 1]
        m_xr = put("sp", [b7], lambda: S.dma_start(xr[:, :, :], x.rearrange("(t p) f -> p t f", p=128)), s_xr, 16)
        m_b2 = put("sp", [b7], lambda: S.dma_start(b2b[:, :], b2.unsqueeze(0).broadcast_to([128, D])), s_b2, 16)
        m_a2 = [put("sp", [b7], lambda i=i, a=a: S.dma_start(a2b[:, i, :], a[0:1, :].broadcast_to([128, D])), s_a2[i], 16)
                for i, a in enumerate((as2, ad2))]
        for c in range(LASTC):
            stage_C(H - 1, c)
            if c + 4 < FT:
                split_w2(H - 1, c + 4)
        for t in range(NT):
            m_xb = put("dve", [m_xr, m_b2], lambda t=t: V.tensor_tensor(xr[:, t, :], xr[:, t, :], b2b[:, :], ALU.add), s_xb)
        evs = {}
        for n in range(6):
            for c in range(LASTC, FT):
                stage_C(H - 1, c, only=n)
            if n in (0, 3):
                continue
            t = {1: 0, 2: 1, 4: 2, 5: 3}[n]
            for (ob, lo, hi), nn in zip(Ocols(t), (n, 3 * (t // 2))):
                evs[t] = put("act", [bank_m[nn], b7], lambda t=t, ob=ob, lo=lo, hi=hi: A.copy(res[:, t, lo:hi], ob), s_h32)
            sums_h(H, t, evs[t], res[:, t, :], a2b, m_a2)
            split_h(H, t, evs[t], res[:, t, :])
        scores_1(H)
        scores_2(H)
        m_sq = put("act", [m_idn], lambda: A.activation(rs[:, 0, 0:1], idn[:, 0:1], ACT.Sqrt), s_rs)
        outv = out.rearrange("(t p) f -> p t f", p=128)
        mr_m = {}
        for d in range(NT):
            pieces = [(O[d][:, 0:512], 0, 512), (O[4 + d % 2][:, 0:256], 512, 768)]
            for t in range(NT):
                for p, (pa, ha, ws) in enumerate(((Ph, hh, [hh_m[H, t], P_m[H][t][0]]), (Pl, hh, [P_m[H][t][1]]), (Ph, hl, [hl_m[H, t]]))):
                    for i, (ob, lo, hi) in enumerate(pieces):
                        end = t == NT - 1 and p == 2
                        m = put("pe", [evs[NT - 1], mr_m.get(d - 2), *ws], lambda d=d, t=t, p=p, pa=pa, ha=ha, ob=ob, lo=lo, hi=hi, i=i, end=end: T.matmul(
                            ob, pa[:, t, 128 * d:128 * d + 128], ha[:, t, lo:hi],
                            start=(t == 0 and p == 0), stop=end),
                            s_D if end and i == 1 else None)
            if d == 0:
                kd, bd, rel = bank()
                for dd in range(NT):
                    m = put("pe", [rel, sm_m[H], m_oner], lambda d=dd: T.matmul(
                        bd[:, 2 * d:2 * d + 2], L[:, 0, 128 * d:128 * d + 128], oner[:, 0:2].bitcast(f32),
                        start=(d == 0), stop=True, skip_group_check=True), s_den if dd == NT - 1 else None)
                dnf = dn[:, :, :].rearrange("p t c -> p (t c)")
                m0 = put("dve", [m], lambda: V.tensor_scalar(dnf, bd[:, 0:2 * NT], EPS, None, ALU.add), s_dn)
                m_dn = put("dve", [m0], lambda: V.reciprocal(dnf, dnf), s_dn)
            for i, (ob, lo, hi) in enumerate(pieces):
                mr = put("dve", [m, m_dn, m_xb, hl_m[H, d]], lambda d=d, ob=ob, lo=lo, hi=hi: V.scalar_tensor_tensor(
                    out=res[:, d, lo:hi], in0=ob, scalar=dn[:, d, 0:1], in1=xr[:, d, lo:hi], op0=ALU.mult, op1=ALU.add), s_res)
            mr_m[d] = mr
            for i in range(2):
                ms = put("dve", [mr], lambda d=d, i=i: V.bn_stats(st6[:, d, i, :], res[:, d, HALF * i:HALF * i + HALF]), s_st)
            mm = put("dve", [ms], lambda d=d: V.bn_aggr(mv[:, d, :], st6[:, d, :, :]), s_mv)
            mv1 = put("dve", [mm], lambda d=d: V.tensor_scalar(rs[:, d, 1:2], mv[:, d, 1:2], LN_EPS, None, ALU.add), s_mv)
            m1 = put("act", [mv1, m_sq], lambda d=d: A.activation(rs[:, d, 0:1], rs[:, d, 1:2], ACT.Sqrt), s_rs)
            m2 = put("dve", [m1], lambda d=d: V.reciprocal(rs[:, d, 1:2], rs[:, d, 0:1]), s_mv)
            mf = put("dve", [m2], lambda d=d: V.tensor_scalar(
                res[:, d, :], res[:, d, :], mv[:, d, 0:1], rs[:, d, 1:2], ALU.subtract, ALU.mult), s_fin)
            last = put("sp", [mf], lambda d=d: S.dma_start(outv[:, d, :], res[:, d, :]), s_out, 16)
        queue["sp"].append(lambda e: e.wait_ge(last[0][1], last[1]))

        with nc.Block() as block:
            def run(name):
                def body(e):
                    for step in queue[name]:
                        step(e)
                return body
            block.sync(run("sp"))
            block.scalar(run("act"))
            block.vector(run("dve"))
            block.gpsimd(run("pool"))
            block.tensor(run("pe"))


def kernel(**inputs):
    import numpy as np
    import concourse.bacc as bacc
    from concourse import mybir as mb
    from concourse.bass_utils import run_bass_kernel_spmd

    nc = bacc.Bacc("TRN2", target_bir_lowering=False, num_devices=1)
    p = "L0_gnn_"
    x = np.asarray(inputs["x"])
    b1 = np.asarray(inputs[p + "b1"])
    given = [("x", x), ("xT", x.T), ("src", inputs["src"]), ("dst", inputs["dst"]), ("W1", inputs[p + "W1"]),
             ("as1", inputs[p + "a_src1"]), ("ad1", inputs[p + "a_dst1"]), ("b1c", b1.reshape(48, 128).T),
             ("W2", inputs[p + "W2"]), ("as2", inputs[p + "a_src2"]), ("ad2", inputs[p + "a_dst2"]),
             ("b2", inputs[p + "b2"])]
    arrays, args = {}, []
    for name, a in given:
        a = np.ascontiguousarray(np.asarray(a))
        arrays[f"in_{name}"] = a
        args.append(nc.dram_tensor(f"in_{name}", a.shape, mb.dt.from_np(a.dtype), kind="ExternalInput").ap())
    o = nc.dram_tensor("out_0", (512, 768), mb.dt.float32, kind="ExternalOutput").ap()
    gat_resnorm_kernel(nc, *args, o)
    r = run_bass_kernel_spmd(nc, [arrays], core_ids=[0])
    return r.results[0]["out_0"]
```

```python
import concourse.bass as bass
from concourse import mybir
from contextlib import ExitStack


def gat_resnorm_kernel(nc, x, xT, src, dst, W1, as1, ad1, b1c, W2, as2, ad2, b2, out):
    f32, f32r, bf16 = mybir.dt.float32, mybir.dt.float32r, mybir.dt.bfloat16
    i32, f16 = mybir.dt.int32, mybir.dt.float16
    ALU, ACT = mybir.AluOpType, mybir.ActivationFunctionType

    N, D, H, E = 512, 768, 8, 16896
    NT, FT = N // 128, D // 128
    HALF = D // 2
    EJ = E // 128
    GROUPS = [27, 27, 26, 26, 26]
    OHR = 11
    FIELD = 4096
    SLOPE, EPS, LN_EPS, BIG = 0.2, 1e-16, 1e-5, 1e30
    NR, N2, NY, LASTC = 5, 4, 3, 3

    queue = {"sp": [], "act": [], "dve": [], "pool": [], "pe": []}
    count, seen = {}, {}
    ctx = ExitStack()
    with ctx:
        def sem(name):
            s = ctx.enter_context(nc.semaphore(name))
            count[name] = 0
            return (name, s)

        def put(eng, waits, fn, done=None, by=1):
            for w in waits:
                if w is None:
                    continue
                (name, s), v = w
                if seen.get((eng, name), 0) < v:
                    seen[eng, name] = v
                    queue[eng].append(lambda e, s=s, v=v: e.wait_ge(s, v))
            if done is None:
                queue[eng].append(lambda e: fn())
                return None
            count[done[0]] += by
            queue[eng].append(lambda e: fn().then_inc(done[1], by))
            return (done, count[done[0]])

        def sb(name, shape, dt, where=ctx):
            return where.enter_context(nc.sbuf_tensor(name, shape, dt))

        V, A, G, T, S = nc.vector, nc.scalar, nc.gpsimd, nc.tensor, nc.sync

        xTh = sb("xTh", [128, FT, N], f32r)
        xTl = sb("xTl", [128, FT, N], f32r)
        CT = sb("CT", [128, NT, N], f32)
        Mk = sb("Mk", [128, NT, N], bf16)
        Wr = sb("Wr", [128, NR, D], f32)
        W2h = sb("W2h", [128, N2, D], f32r)
        W2l = sb("W2l", [128, N2, D], f32r)
        h32 = sb("h32", [128, 2, D], f32)
        hh = sb("hh", [128, NT, D], f32r)
        hl = sb("hl", [128, NT, D], f32r)
        abc = sb("abc", [128, 2, 2, D], f32)
        rb = sb("rb", [128, N], f32)
        idn = sb("idn", [128, 128], f32)
        oner = sb("oner", [128, 2], f32r)
        b1s = sb("b1s", [128, H * FT], f32)
        asd = sb("asd", [128, 2, 2, NT], f32)
        amx = sb("amx", [128, NT], f32)
        zm = sb("zm", [128, NT], f32)
        mc = sb("mc", [128, NT], f32)
        r12 = sb("r12", [128, 2, NT], f32)
        as02 = sb("as02", [128, NT], f32)
        junk = sb("junk", [128, D], bf16)
        with ExitStack() as c1:
            W1h = sb("W1h", [128, FT, D], f32r, c1)
            W1l = sb("W1l", [128, FT, D], f32r, c1)
        c2 = ctx.enter_context(ExitStack())
        xr = sb("xr", [128, NT, D], f32, c2)
        res = sb("res", [128, NT, D], f32, c2)
        b2b = sb("b2b", [128, D], f32, c2)
        a2b = sb("a2b", [128, 2, D], f32, c2)
        st6 = sb("st6", [128, NT, 2, 6], f32, c2)
        mv = sb("mv", [128, NT, 2], f32, c2)
        rs = sb("rs", [128, NT, 2], f32, c2)
        dn = sb("dn", [128, NT, 2], f32, c2)
        epc = sb("epc", [128, 1], f32, c2)
        prt = sb("prt", [128, 2, 2, 2], f32, c2)
        junk2 = sb("junk2", [128, D], bf16, c2)
        sb("pad", [128, 9216 - (2 * NT * D + 3 * D + NT * 12 + 3 * NT * 2 + 16 + D // 2)], f32, c2)
        with ExitStack() as c3:
            si = sb("si", [128, EJ], i32, c3)
            di = sb("di", [128, EJ], i32, c3)
            up = sb("up", [128, EJ], f32, c3)
            df = sb("df", [128, EJ], f32, c3)
            uf = sb("uf", [128, EJ], f32, c3)
            wf = sb("wf", [128, EJ], f32, c3)
            nuf = sb("nuf", [128, EJ], f32, c3)
            nwf = sb("nwf", [128, EJ], f32, c3)
            dist = sb("dist", [128, 2, 256], f16, c3)
            ioi = sb("ioi", [128, N], i32, c3)
            iof = sb("iof", [128, N], f16, c3)
            ohd = sb("ohd", [128, OHR, N], bf16, c3)
            ohs = sb("ohs", [128, OHR, 256], bf16, c3)
            ji = sb("ji", [128, 2, 2, N], i32, c3)
            jf = sb("jf", [128, 2, 2, N], i32, c3)
            cnt = sb("cnt", [128, 2, 2, N], i32, c3)
        L = sb("L", [128, NT, N], f32)
        Ph = sb("Ph", [128, NT, N], f32r)
        Pl = sb("Pl", [128, NT, N], f32r)
        y2 = sb("y2", [128, N], f32)
        gh = sb("gh", [128, FT, N], f32r)
        gl = sb("gl", [128, FT, N], f32r)

        ys = [L[:, 0, :], L[:, 1, :], y2[:, :]]
        exs = [L[:, 2, :], L[:, 3, :]]

        O = [ctx.enter_context(nc.psum_tensor(f"O{i}", [128, 512], f32)) for i in range(6)]
        R = [ctx.enter_context(nc.psum_tensor(f"R{i}", [128, 512], f32)) for i in range(2)]

        def Ocols(t):
            return [(O[t][:, 0:512], 0, 512), (O[4 + t // 2][:, 256 * (t % 2):256 * (t % 2) + 256], 512, 768)]

        ring = {"k": 0, "rel": [None, None]}

        def bank():
            k = ring["k"] % 2
            ring["k"] += 1
            return k, R[k], ring["rel"][k]

        s_edge, s_b1, s_out = sem("s_edge"), sem("s_b1"), sem("s_out")
        s_edg2 = sem("s_edg2")
        s_wr = [sem(f"s_wr{i}") for i in range(NR)]
        s_abc = [sem(f"s_abc{i}") for i in range(4)]
        s_xr, s_b2, s_a2 = sem("s_xr"), sem("s_b2"), [sem("s_a20"), sem("s_a21")]
        s_io, s_cst, s_iof, s_key = sem("s_io"), sem("s_cst"), sem("s_iof"), sem("s_key")
        s_ds, s_os, s_oh, s_hist, s_ji, s_jf, s_cnt, s_CT = (sem(n) for n in ("s_ds", "s_os", "s_oh", "s_hist", "s_ji", "s_jf", "s_cnt", "s_CT"))
        s_CTt, s_mk = sem("s_CTt"), sem("s_mk")
        s_xh, s_xl, s_w1h, s_w1l, s_w2h, s_w2l = (sem(n) for n in ("s_xh", "s_xl", "s_w1h", "s_w1l", "s_w2h", "s_w2l"))
        s_B, s_h32, s_hh, s_hl, s_asd = (sem(n) for n in ("s_B", "s_h32", "s_hh", "s_hl", "s_asd"))
        s_Pd, s_sd, s_sm, s_lk, s_bc, s_amx, s_zm, s_mc, s_L, s_exp = (sem(n) for n in ("s_Pd", "s_sd", "s_sm", "s_lk", "s_bc", "s_amx", "s_zm", "s_mc", "s_L", "s_exp"))
        s_P, s_Ph, s_Pl, s_den, s_rb0, s_rb = (sem(n) for n in ("s_P", "s_Ph", "s_Pl", "s_den", "s_rb0", "s_rb"))
        s_glg, s_nu, s_hlg, s_smh, s_sml, s_r12, s_as02 = sem("s_glg"), sem("s_nu"), sem("s_hlg"), sem("s_smh"), sem("s_sml"), sem("s_r12"), sem("s_as02")
        s_A, s_y, s_ex, s_em, s_g, s_gh, s_gl, s_C = (sem(n) for n in ("s_A", "s_y", "s_ex", "s_em", "s_g", "s_gh", "s_gl", "s_C"))
        s_xb, s_D, s_dn, s_res, s_st, s_mv, s_rs, s_fin = (sem(n) for n in ("s_xb", "s_D", "s_dn", "s_res", "s_st", "s_mv", "s_rs", "s_fin"))

        m_src = put("sp", [], lambda: S.dma_start(si[:, :], src.rearrange("(p j) -> p j", p=128)), s_edge, 16)
        m_dst = put("sp", [], lambda: S.dma_start(di[:, :], dst.rearrange("(p j) -> p j", p=128)), s_edg2, 16)
        m_b1 = put("sp", [], lambda: S.dma_start(b1s[:, :], b1c), s_b1, 16)

        raw = {"n": 0, "free": [None] * NR}

        def load_raw(rows, width=D):
            n = raw["n"] % NR
            raw["n"] += 1
            m = put("sp", [raw["free"][n]], lambda: S.dma_start(Wr[:, n, 0:width], rows), s_wr[n], 16)
            return n, m

        w1_m, w2_m = {}, {}
        B_done, C_done, A_done = {}, {}, {}

        def split_w1(h, k):
            n, m = load_raw(W1[128 * k:128 * k + 128, D * h:D * h + D])
            mh = put("act", [m, B_done.get(h - 1), *(W1_free if h == 2 else [])], lambda: A.copy(W1h[:, k, :], Wr[:, n, :]), s_w1h)
            ml = put("pool", [m, mh, B_done.get(h - 1), *(W1_free if h == 2 else [])],
                     lambda: G.tensor_tensor(W1l[:, k, :], Wr[:, n, :], W1h[:, k, :].bitcast(f32), ALU.subtract), s_w1l)
            raw["free"][n] = ml
            w1_m[h, k] = [mh, ml]

        w2 = {"n": 0, "free": [None] * N2}

        def split_w2(h, k):
            n, m = load_raw(W2[D * h + 128 * k:D * h + 128 * k + 128, :])
            q = w2["n"] % N2
            w2["n"] += 1
            mh = put("act", [m, w2["free"][q]], lambda: A.copy(W2h[:, q, :], Wr[:, n, :]), s_w2h)
            ml = put("pool", [m, mh, w2["free"][q]],
                     lambda: G.tensor_tensor(W2l[:, q, :], Wr[:, n, :], W2h[:, q, :].bitcast(f32), ALU.subtract), s_w2l)
            raw["free"][n] = ml
            w2_m[h, k] = (q, [mh, ml])

        abc_m, as_done = {}, {}

        def load_abc(h):
            abc_m[h] = [
                put("sp", [as_done.get(h - 2)],
                    lambda a=a, i=i: S.dma_start(abc[:, h % 2, i, :], a[h:h + 1, :].broadcast_to([128, D])),
                    s_abc[2 * (h % 2) + i], 16)
                for i, a in enumerate((as1, ad1))]

        m_io = put("pool", [], lambda: G.iota(ioi[:, :], pattern=[[1, N]], base=0, channel_multiplier=0), s_io)
        m_z = put("pool", [], lambda: G.memset(idn[:, :], 0.0), s_cst)
        m_idn = put("pool", [m_z], lambda: G.affine_select(
            out=idn[:, :], in_=idn[:, :], compare_op=ALU.not_equal, fill=1.0, base=0,
            pattern=[[-1, 128]], channel_multiplier=1), s_cst)
        m_oner = put("pool", [m_idn], lambda: G.tensor_scalar(oner[:, :], idn[:, 0:2], 0.0, 1.0, ALU.mult, ALU.add), s_cst)

        m_iof = put("dve", [m_io], lambda: V.tensor_copy(iof[:, :], ioi[:, :]), s_iof)
        m_df = put("dve", [m_dst], lambda: V.tensor_copy(df[:, :], di[:, :]), s_key)
        m_up = put("dve", [m_src], lambda: V.tensor_scalar(up[:, :], si[:, :], 256.0, 1.0, ALU.is_ge, ALU.mult), s_key)
        put("dve", [m_up], lambda: V.scalar_tensor_tensor(
            out=uf[:, :], in0=up[:, :], scalar=-256.0, in1=si[:, :], op0=ALU.mult, op1=ALU.add), s_key)
        m_key = put("dve", [], lambda: V.tensor_scalar(wf[:, :], up[:, :], float(FIELD - 1), 1.0, ALU.mult, ALU.add), s_key)

        put("act", [m_idn], lambda: A.activation(as02[:, 0:1], idn[:, 0:1], ACT.Abs), s_as02)
        m_nu = put("act", [m_key], lambda: A.mul(nuf[:, :], uf[:, :], -1.0), s_nu)
        m_nw = put("act", [m_key], lambda: A.mul(nwf[:, :], wf[:, :], -1.0), s_nu)

        def split_x(k):
            n, m = load_raw(xT[128 * k:128 * k + 128, :], N)
            mh = put("act", [m], lambda: A.copy(xTh[:, k, :], Wr[:, n, 0:N]), s_xh)
            ml = raw["free"][n] = put("pool", [mh, m], lambda: G.tensor_tensor(
                xTl[:, k, :], Wr[:, n, 0:N], xTh[:, k, :].bitcast(f32), ALU.subtract), s_xl)
            return mh, ml

        load_abc(0)
        x_m = []

        hist = {}
        acts = {"n": 0, 0: None, 1: None}
        m_ji, m_jf, m_cnt, m_grp = {}, {}, {}, {}

        def evict(g):
            for b in range(2):
                m_ji[g] = put("act", [m_grp[g], m_jf.get(g - 2)],
                              lambda b=b: A.copy(ji[:, g % 2, b, :], O[2 * (g % 2) + b][:, :]), s_ji)

        def decode(g):
            to = cnt if g == 0 else jf
            m_jf[g] = None
            put("dve", [m_ji[g], m_cnt.get(g - 1)], lambda: V.tensor_scalar(
                to[:, 0, :, :], ji[:, g % 2, :, :], FIELD - 1, None, ALU.bitwise_and), s_jf)
            m_jf[g] = put("dve", [], lambda: V.tensor_scalar(
                to[:, 1, :, :], ji[:, g % 2, :, :], 12, None, ALU.logical_shift_right), s_jf)
            if 0 < g < len(GROUPS) - 1:
                m_cnt[g] = put("pool", [m_jf[g], m_jf[0], m_cnt.get(g - 1)], lambda: G.tensor_tensor(
                    cnt[:, :, :, :], cnt[:, :, :, :], jf[:, :, :, :], ALU.add), s_cnt)

        starts = [sum(GROUPS[:g]) for g in range(len(GROUPS) + 1)]
        oh_m = {}

        def make(j):
            if j >= EJ:
                return
            r, old = j % OHR, hist.get(j - OHR)
            m_d = put("dve", [m_iof, m_df, old], lambda: V.tensor_scalar(
                ohd[:, r, :], iof[:, :], df[:, j:j + 1], None, ALU.is_equal), s_oh)
            if j % 8 in ((2, 6) if j < 52 else (2, 4, 7)):
                z = acts["n"] % 2
                acts["n"] += 1
                m_ds = put("act", [m_iof, m_nw, acts[z]], lambda: A.activation(
                    dist[:, z, :], iof[:, 0:256], ACT.Abs, bias=nuf[:, j:j + 1], scale=1.0), s_ds)
                m_s = acts[z] = put("act", [m_ds, old], lambda: A.activation(
                    ohs[:, r, :], dist[:, z, :], ACT.Relu, bias=wf[:, j:j + 1], scale=nwf[:, j:j + 1]), s_os)
            else:
                m_s = put("dve", [m_key, m_iof, old], lambda: V.tensor_scalar(
                    ohs[:, r, :], iof[:, 0:256], uf[:, j:j + 1], wf[:, j:j + 1], ALU.is_equal, ALU.mult), s_oh)
            oh_m[j] = [m_d, m_s]

        def count_block(j):
            g = max(i for i in range(len(GROUPS)) if starts[i] <= j)
            r, first, last = j % OHR, j == starts[g], j == starts[g + 1] - 1
            for q in range(2):
                hist[j] = m_grp[g] = put("pe", [*oh_m[j], m_ji.get(g - 2)], lambda q=q: T.matmul(
                    O[2 * (g % 2) + q][:, :], ohs[:, r, 128 * q:128 * q + 128], ohd[:, r, :], start=first, stop=last), s_hist)

        sm_m, L_free = {}, [None, None]
        hl_m, hh_m, h32_free, asd_m, P_m, rb_m, r12_m, as02_m = {}, {}, [None, None], {}, {}, {}, {}, {}
        own_free, gh_m, gl_m, y_free, ex_free = [], {}, {}, [None] * NY, [None, None]

        def sums_h(h, t, ready, get, a_ap, m_a):
            for i in range(2):
                two = h == H and i
                m = put("dve", [ready, m_a[i], as_done.get("junk", [None, None])[two]], lambda i=i, two=two: V.tensor_tensor_reduce(
                    out=(junk2 if two else junk)[:, :], in0=get, in1=a_ap[:, i, :], op0=ALU.mult, op1=ALU.add, scale=1.0, scalar=0.0,
                    accum_out=asd[:, h % 2, i, t:t + 1]), s_asd)
                as_done.setdefault("junk", [None, None])[two] = m
            asd_m[h] = as_done[h] = m

        def high_h(h, t, ready, get):
            hh_m[h, t] = put("act", [ready, A_done.get(h - 1)], lambda: A.copy(hh[:, t, :], get), s_hh)

        def low_h(h, t, get, low="dve"):
            mine = V if low == "dve" else G
            hl_m[h, t] = put(low, [hh_m[h, t], A_done.get(h - 1)], lambda: mine.tensor_tensor(
                hl[:, t, :], get, hh[:, t, :].bitcast(f32), ALU.subtract), s_hl if low == "dve" else s_hlg)

        def split_h(h, t, ready, get):
            high_h(h, t, ready, get)
            low_h(h, t, get)

        h32_m = {}

        def half_B(h, t, c, own=None, between=None):
            k, bk, rel = bank() if own is None else (None, *own)
            for f in range(FT):
                if between and f == 3:
                    between()
                for p, (xa, wa) in enumerate(((xTh, W1h), (xTh, W1l), (xTl, W1h))):
                    end = f == FT - 1 and p == 2
                    m = put("pe", [rel, *x_m[f], w1_m[h, f][0], w1_m[h, f][1] if p else None],
                            lambda xa=xa, wa=wa, f=f, p=p, end=end: T.matmul(
                                bk[:, 0:HALF], xa[:, f, 128 * t:128 * t + 128], wa[:, f, HALF * c:HALF * c + HALF],
                                start=(f == 0 and p == 0), stop=end), s_B if end else None)
            B_done[h] = m
            if own is not None:
                return
            h32_m[h, t] = ring["rel"][k] = put("act", [m, h32_free[t % 2]], lambda: A.copy(
                h32[:, t % 2, HALF * c:HALF * c + HALF], bk[:, 0:HALF]), s_h32)

        def sums_B(h, t):
            sums_h(h, t, h32_m[h, t], h32[:, t % 2, :], abc[:, h % 2, :, :], abc_m[h])

        def split_B(h, t):
            split_h(h, t, h32_m[h, t], h32[:, t % 2, :])
            h32_free[t % 2] = hl_m[h, t]

        def bcast(col, m, tiles=range(NT), own=None):
            k, bk, rel = bank() if own is None else (None, *own)
            for t in tiles:
                mk = put("pe", [rel, m, m_idn], lambda t=t: T.transpose(
                    bk[:, 128 * t:128 * t + 128], col[:, t:t + 1].broadcast_to([128, 128]), idn[:, :]),
                    s_bc if t == tiles[-1] else None)
            return k, bk, mk

        def scores_1(h, parts=((0, NT),)):
            par = h % 2
            ks, bs, ms = bcast(asd[:, par, 0, :], asd_m[h])
            as02_m[h] = put("act", [asd_m[h]], lambda: A.mul(as02[:, :], asd[:, par, 0, :], SLOPE), s_as02)
            for lo, hi in parts:
                for t in range(lo, hi):
                    m = put("dve", [ms, m_mk[t], A_done.get(h - 1)], lambda t=t: V.tensor_tensor_reduce(
                        out=Pl[:, t, :], in0=bs[:, :], in1=Mk[:, t, :], op0=ALU.add, op1=ALU.max, scale=1.0, scalar=-3e38,
                        accum_out=amx[:, t:t + 1]), s_amx)
                ad = asd[:, par, 1, lo:hi]
                mz = put("dve", [m], lambda lo=lo, hi=hi, ad=ad: V.tensor_tensor(zm[:, lo:hi], amx[:, lo:hi], ad, ALU.add), s_zm)
                mm = put("dve", [mz], lambda lo=lo, hi=hi: V.scalar_tensor_tensor(
                    out=mc[:, lo:hi], in0=zm[:, lo:hi], scalar=SLOPE, in1=zm[:, lo:hi], op0=ALU.mult, op1=ALU.max), s_mc)
                put("dve", [mm], lambda lo=lo, hi=hi, ad=ad: V.tensor_tensor(r12[:, 0, lo:hi], ad, mc[:, lo:hi], ALU.subtract), s_r12)
                r12_m[h, lo] = put("dve", [mm], lambda lo=lo, hi=hi, ad=ad: V.scalar_tensor_tensor(
                    out=r12[:, 1, lo:hi], in0=ad, scalar=SLOPE, in1=mc[:, lo:hi], op0=ALU.mult, op1=ALU.subtract), s_r12)
            ring["rel"][ks] = m

        def scores_2(h, part=(0, NT), own=(None, None)):
            par = h % 2
            lo, hi = part
            d0, d1 = 128 * lo, 128 * hi
            k2, b2k, m2 = bcast(r12[:, 1, :], r12_m[h, lo], range(lo, hi), own[1])
            k1, b1k, m1 = bcast(r12[:, 0, :], r12_m[h, lo], range(lo, hi), own[0])
            first = h == 0
            P = P_m[h, lo] = []
            mS = []
            for u in range(NT + 2):
                if u < NT:
                    mI = put("act", [m2, as02_m[h], *L_free], lambda t=u: A.activation(
                        L[:, t, d0:d1], b2k[:, d0:d1], ACT.Identity, bias=as02[:, t:t + 1], scale=1.0), s_L)
                    mS.append(put("dve", [m1, mI], lambda t=u: V.scalar_tensor_tensor(
                        out=L[:, t, d0:d1], in0=b1k[:, d0:d1], scalar=asd[:, par, 0, t:t + 1], in1=L[:, t, d0:d1], op0=ALU.add, op1=ALU.max), s_lk))
                if 1 <= u <= NT:
                    mE = put("act", [mS[u - 1]], lambda t=u - 1: A.activation(L[:, t, d0:d1], L[:, t, d0:d1], ACT.Exp), s_exp)
                    mP = put("dve", [mE], lambda t=u - 1: V.scalar_tensor_tensor(
                        out=L[:, t, d0:d1], in0=L[:, t, d0:d1], scalar=1.0, in1=CT[:, t, d0:d1], op0=ALU.min, op1=ALU.mult), s_P)
                    P.append([None, mP])
                    if first and u in (2, 4):
                        sm = put("dve", [mP, P[u - 2][1]], lambda u=u: V.tensor_tensor(
                            (y2, rb)[u // 2 - 1][:, :], L[:, u - 2, :], L[:, u - 1, :], ALU.add), s_sd)
                if u >= 2:
                    t = u - 2
                    P[t][0] = put("act", [P[t][1], A_done.get(h - 1)], lambda t=t: A.copy(Ph[:, t, d0:d1], L[:, t, d0:d1]), s_Ph)
            for k, m in ((k2, mI), (k1, mS[-1])):
                if k is None:
                    own_free.append(m)
                else:
                    ring["rel"][k] = m
            if first:
                sm_m[h] = put("dve", [sm], lambda: V.tensor_tensor(y2[:, :], y2[:, :], rb[:, :], ALU.add), s_sd)
                split_sum(h)
            for t in range(NT):
                low, mine = ("dve", V) if h in (0, H) and t % 2 else ("pool", G)
                P[t][1] = put(low, [P[t][1], P[t][0], A_done.get(h - 1)], lambda t=t, mine=mine: mine.tensor_tensor(
                    Pl[:, t, d0:d1], L[:, t, d0:d1], Ph[:, t, d0:d1].bitcast(f32), ALU.subtract), s_Pl if mine is G else s_Pd)
            if first:
                return
            low, mine = ("dve", V) if h == 1 else ("pool", G)
            sm = None
            for a, b in ((0, 1), (2, 3), (0, 2)):
                sm = put(low, [*P[a], *P[b], sm], lambda a=a, b=b: mine.tensor_tensor(
                    L[:, a, d0:d1], L[:, a, d0:d1], L[:, b, d0:d1], ALU.add), s_sm if mine is G else s_sd)
            if h < H:
                sm_m[h] = sm
            else:
                sm_m[h, lo] = sm

        def split_sum(h):
            total = L[:, 0, :] if h else y2[:, :]
            mh = put("act", [sm_m[h], C_done.get((h - 1, 0))], lambda: A.copy(gh[:, 0, :], total), s_smh)
            ml = put("dve", [mh, sm_m[h], C_done.get((h - 1, 0))], lambda: V.tensor_tensor(
                gl[:, 0, :], total, gh[:, 0, :].bitcast(f32), ALU.subtract), s_sml)
            sm_m[h] = [mh, ml]

        def denom(h):
            k, bk, rel = bank() if h else (None, O[4], None)
            for i in range(2):
                m = put("pe", [rel, sm_m[h][i], m_oner], lambda i=i: T.matmul(
                    bk[:, :], oner[:, 0:1].broadcast_to([128, 128]), (gh, gl)[i][:, 0, :], start=(i == 0), stop=(i == 1)), s_den if i else None)
            m0 = put("dve", [m], lambda: V.tensor_scalar(rb[:, :], bk[:, :], EPS, None, ALU.add), s_rb0)
            if h:
                ring["rel"][k] = m0
            else:
                O_free.append(m0)
            rb_m[h] = put("dve", [m0], lambda: V.reciprocal(rb[:, :], rb[:, :]), s_rb)

        y_m, A_m, A_bank = {}, {}, {}

        def stage_A(h, c, between=None):
            k, bk, rel = bank()
            for t in range(NT):
                if t == 0 and between:
                    between()
                P = P_m[h, 0]
                passes = ((hh, Ph, [hh_m[h, t], P[t][0]]), (hh, Pl, [P[t][1]]), (hl, Ph, [hl_m[h, t]]))
                for p, (ha, pa, ws) in enumerate(passes):
                    m = put("pe", [rel, *ws], lambda ha=ha, pa=pa, t=t, p=p: T.matmul(
                        bk[:, :], ha[:, t, 128 * c:128 * c + 128], pa[:, t, :],
                        start=(t == 0 and p == 0), stop=(t == NT - 1 and p == 2)),
                        s_A if (t == NT - 1 and p == 2) else None)
            A_done[h] = A_m[h, c] = m
            A_bank[h, c] = k, bk

        def keep_A(h, c):
            k, bk = A_bank[h, c]
            m = A_m[h, c]
            my = put("dve", [m, rb_m[h], y_free[c % NY]], lambda: V.tensor_tensor(ys[c % NY], bk[:, :], rb[:, :], ALU.mult), s_y)
            ring["rel"][k] = my
            col = h * FT + c
            y_m[h, c] = put("act", [my, m_b1, ex_free[c % 2]], lambda: A.activation(
                exs[c % 2], ys[c % NY], ACT.Exp, bias=b1s[:, col:col + 1], scale=1.0), s_ex)

        def elu(h, c):
            yt, et = ys[c % NY], exs[c % 2]
            col = h * FT + c
            me = put("dve", [y_m[h, c]], lambda: V.tensor_scalar(et, et, 1.0, 1.0, ALU.min, ALU.subtract), s_em)
            mg = put("dve", [me, m_b1], lambda: V.scalar_tensor_tensor(
                out=yt, in0=yt, scalar=b1s[:, col:col + 1], in1=et, op0=ALU.add, op1=ALU.max), s_g)
            ex_free[c % 2] = L_free[1] = mg
            gh_m[h, c] = put("act", [mg, C_done.get((h - 1, c))], lambda: A.copy(gh[:, c, :], yt), s_gh)

        def elu_low(h, c):
            low, mine = ("dve", V) if h else ("pool", G)
            gl_m[h, c] = put(low, [gh_m[h, c], C_done.get((h - 1, c))], lambda: mine.tensor_tensor(
                gl[:, c, :], ys[c % NY], gh[:, c, :].bitcast(f32), ALU.subtract), s_gl if h else s_glg)
            y_free[c % NY] = L_free[0] = gl_m[h, c]

        PIECES = [[p for t in (0, 1) for p in [(t, *Ocols(t)[1])]], [(0, *Ocols(0)[0])], [(1, *Ocols(1)[0])],
                  [p for t in (2, 3) for p in [(t, *Ocols(t)[1])]], [(2, *Ocols(2)[0])], [(3, *Ocols(3)[0])]]
        bank_m = {}

        def stage_C(h, c, only=None, between=None):
            q, ws = w2_m[h, c]
            for p, (ga, wa) in enumerate(((gh, W2h), (gh, W2l), (gl, W2h))):
                if between and p == 1:
                    between()
                for n, group in enumerate(PIECES):
                    for t, ob, lo, hi in group:
                        if only not in (None, n):
                            continue
                        first, last = (h == 0 and c == 0 and p == 0), (h == H - 1 and c == FT - 1 and p == 2)
                        m = put("pe", [ws[0], ws[1] if p else None, gh_m[h, c], gl_m[h, c] if p == 2 else None, *(O_free if h == 0 and c == 0 else [])],
                                lambda ga=ga, wa=wa, t=t, ob=ob, lo=lo, hi=hi, first=first, last=last: T.matmul(
                                    ob, ga[:, c, 128 * t:128 * t + 128], wa[:, q, lo:hi],
                                    start=first and (hi - lo == 512 or t % 2 == 0), stop=last, skip_group_check=True),
                                s_C if p == 2 and t == group[-1][0] and n == (5 if only is None else only) else None)
            C_done[h, c] = w2["free"][q] = m
            if only is not None:
                bank_m[only] = m

        def counts_end():
            g = len(GROUPS) - 1
            evict(g)
            decode(g)
            cv = CT[:, :, :].rearrange("p (f b) n -> p f b n", f=2)
            for i in range(2):
                m = put("dve", [m_cnt[g - 1], m_jf[g]], lambda i=i: V.tensor_tensor(
                    cv[:, i, :, :], cnt[:, i, :, :], jf[:, i, :, :], ALU.add), s_CT)
            return m

        def masks():
            out_m = []
            for d in range(NT):
                for s in range(NT):
                    m = put("pe", [m_CT, m_idn, m_ji[len(GROUPS) - 1]], lambda d=d, s=s: T.transpose(
                        O[d][:, 128 * s:128 * s + 128], CT[:, s, 128 * d:128 * d + 128], idn[:, :]),
                        s_CTt if s == NT - 1 else None)
                out_m.append(put("dve", [m], lambda d=d: V.tensor_scalar(
                    Mk[:, d, :], O[d][:, :], 0.0, -BIG, ALU.is_equal, ALU.mult), s_mk))
            return out_m

        def mix(h, steps):
            for c in range(FT):
                if h or c > 1:
                    stage_A(h, c)
                keep_A(h, c)
                if c > 1:
                    elu_low(h, c - 2)
                if c:
                    elu(h, c - 1)
                for step in steps.get(c, []):
                    step[0](*step[1:])
            elu(h, FT - 1)
            elu_low(h, FT - 2)
            elu_low(h, FT - 1)

        load_abc(1)
        EV, DE = 4, 12
        B_AT = [54 + 6 * i for i in range(8)]
        W_AT = [97 + 4 * i for i in range(6)]
        for j in range(OHR):
            make(j)
        for j in range(EJ):
            if j in B_AT:
                t, c = divmod(B_AT.index(j), 2)
                half_B(0, t, c)
                if c:
                    sums_B(0, t)
                    split_B(0, t)
            count_block(j)
            make(j + OHR)
            if j - EV in starts[1:5]:
                evict(starts.index(j - EV) - 1)
            if j - DE in starts[1:5]:
                decode(starts.index(j - DE) - 1)
            if j % 4 == 1 and j // 4 < 2 * FT:
                k = j // 8
                if j % 8 == 1:
                    x_m.append(split_x(k))
                else:
                    split_w1(0, k)
            if j in W_AT:
                split_w1(1, W_AT.index(j))
        m_CT = counts_end()
        for t in range(NT):
            for c in range(2):
                n = 2 * t + c
                if n == 3:
                    m_mk = masks()
                    scores_1(0)
                if n == 4:
                    sums_B(1, 0)
                half_B(1, t, c, None if t < 2 else (O[n - 4], m_mk[n - 4]), (lambda: scores_2(0)) if n == 4 else None)
        O_free = []
        for t in (2, 3):
            for c in range(2):
                O_free.append(put("act", [B_done[1]], lambda t=t, c=c: A.copy(
                    res[:, t, HALF * c:HALF * c + HALF], O[2 * t - 4 + c][:, 0:HALF]), s_h32))
        O_m = list(O_free)
        stage_A(0, 0, lambda: denom(0))
        stage_A(0, 1)

        def sums_late(t):
            sums_h(1, t, O_m[-1], res[:, t, :], abc[:, 1, :, :], abc_m[1])

        beside = {1: [(sums_B, 1, 1)], 2: [(sums_late, 2)], 3: [(sums_late, 3)]}
        mix(0, {c: ([(split_w2, 0, c)] if c < N2 else []) + beside.get(c, []) for c in range(FT)})
        for h in range(1, H):
            if h + 1 < H:
                load_abc(h + 1)
            for t in range(NT if h > 1 else 0):
                for c in range(2):
                    half_B(h, t, c)
                sums_B(h, t)
                split_B(h, t)
                split_w2(h - 1, t)
            for c in range(FT):
                stage_C(h - 1, c, None, (lambda: scores_2(1)) if h == 1 and c == 2 else None)
                if c == 0:
                    scores_1(h)
                if c + 4 < FT:
                    split_w2(h - 1, c + 4)
                if c == 1 and h > 1:
                    scores_2(h)
                if h == 1 and c == 2:
                    held = [h32[:, 0, :], h32[:, 1, :], res[:, 2, :], res[:, 3, :]]
                    for t in range(NT):
                        high_h(1, t, h32_m[1, t] if t < 2 else O_m[-1], held[t])
                    split_sum(1)
                    for t in range(NT):
                        low_h(1, t, held[t])
                    h32_free = [hl_m[1, 0], hl_m[1, 1]]
                    W1_free = [hl_m[1, 2], hl_m[1, 3]]
                if c > 1 and h > 1 and h + 1 < H:
                    split_w1(h + 1, c - 2)
            if h > 1:
                split_sum(h)
            for k in range(4 if h == 1 else 0):
                split_w1(h + 1, k)
            denom(h)
            if h + 1 < H:
                mix(h, {0: [(split_w1, h + 1, 4)], 1: [(split_w1, h + 1, 5)]})
            else:
                mix(h, {c: [(split_w2, h, c)] for c in range(N2)})

        b7 = B_done[H - 1]
        m_xr = put("sp", [b7], lambda: S.dma_start(xr[:, :, :], x.rearrange("(t p) f -> p t f", p=128)), s_xr, 16)
        m_b2 = put("sp", [b7], lambda: S.dma_start(b2b[:, :], b2.unsqueeze(0).broadcast_to([128, D])), s_b2, 16)
        m_a2 = [put("sp", [b7], lambda i=i, a=a: S.dma_start(a2b[:, i, :], a[0:1, :].broadcast_to([128, D])), s_a2[i], 16)
                for i, a in enumerate((as2, ad2))]
        for c in range(LASTC):
            stage_C(H - 1, c)
            if c + 4 < FT:
                split_w2(H - 1, c + 4)
        for t in range(NT):
            m_xb = put("dve", [m_xr, m_b2], lambda t=t: V.tensor_tensor(xr[:, t, :], xr[:, t, :], b2b[:, :], ALU.add), s_xb)
        evs = {}
        m_eps = put("pool", [b7], lambda: G.memset(epc[:, :], LN_EPS), s_cst)

        def part_sums(t, j, m, get, lo, hi):
            for i in range(2):
                as_done["junk"][i] = put("dve", [m, m_a2[i], as_done["junk"][i]], lambda i=i: V.tensor_tensor_reduce(
                    out=(junk, junk2)[i][:, lo:hi], in0=get, in1=a2b[:, i, lo:hi], op0=ALU.mult, op1=ALU.add, scale=1.0, scalar=0.0,
                    accum_out=prt[:, t - 2, j, i:i + 1]), s_asd)
            return as_done["junk"][1]

        for n in range(6):
            for c in range(LASTC, FT):
                stage_C(H - 1, c, only=n)
            if n in (1, 2):
                t = n - 1
                for (ob, lo, hi), nn in reversed(list(zip(Ocols(t), (n, 0)))):
                    evs[t] = put("act", [bank_m[nn], b7], lambda t=t, ob=ob, lo=lo, hi=hi: A.copy(res[:, t, lo:hi], ob), s_h32)
                sums_h(H, t, evs[t], res[:, t, :], a2b, m_a2)
                high_h(H, t, evs[t], res[:, t, :])
                low_h(H, t, res[:, t, :], "pool")
            if n == 3:
                for t in (2, 3):
                    evs[t] = put("act", [bank_m[n], b7], lambda t=t: A.copy(res[:, t, 512:768], Ocols(t)[1][0]), s_h32)
                for t in (2, 3):
                    part_sums(t, 1, evs[t], res[:, t, 512:768], 512, 768)
            if n in (4, 5):
                t = n - 2
                m = part_sums(t, 0, bank_m[n], O[t][:, 0:512], 0, 512)
                asd_m[H] = put("dve", [m], lambda t=t: V.tensor_tensor(
                    asd[:, H % 2, :, t], prt[:, t - 2, 0, :], prt[:, t - 2, 1, :], ALU.add), s_asd)
                evs[t] = put("act", [m, bank_m[n]], lambda t=t: A.copy(res[:, t, 0:512], O[t][:, 0:512]), s_h32)
                high_h(H, t, evs[t], res[:, t, :])
                low_h(H, t, res[:, t, :], "pool")
        scores_1(H, ((0, 2), (2, 4)))
        scores_2(H, (0, 2), ((O[2], evs[2]), (O[3], evs[3])))
        scores_2(H, (2, 4))
        m_sq = put("act", [m_idn], lambda: A.activation(rs[:, 0, 0:1], idn[:, 0:1], ACT.Sqrt), s_rs)
        outv = out.rearrange("(t p) f -> p t f", p=128)
        mr_m = {}
        D_m = {}

        def stage_D(d, t, i):
            ob, lo, hi = D_pieces(d)[i]
            P = P_m[H, 2 * (d // 2)]
            for p, (pa, ha, ws) in enumerate(((Ph, hh, [hh_m[H, t], P[t][0]]), (Ph, hl, [hl_m[H, t]]), (Pl, hh, [P[t][1]]))):
                end = t == NT - 1 and p == 2
                D_m[d, i] = put("pe", [evs[NT - 1], mr_m.get(d - 2) if i else None, *(own_free if d > 1 else []), *ws], lambda p=p, pa=pa, ha=ha, end=end: T.matmul(
                    ob, pa[:, t, 128 * d:128 * d + 128], ha[:, t, lo:hi], start=(t == 0 and p == 0), stop=end),
                    s_D if end else None)

        def D_pieces(d):
            return [(O[d][:, 0:512], 0, 512), (O[4 + d % 2][:, 0:256], 512, 768)]

        def tail_denom(lo):
            kd, bd, rel = bank()
            for d in range(lo, lo + 2):
                m = put("pe", [rel, sm_m[H, lo], m_oner], lambda d=d: T.matmul(
                    bd[:, 2 * d:2 * d + 2], L[:, 0, 128 * d:128 * d + 128], oner[:, 0:2].bitcast(f32),
                    start=(d == lo), stop=True, skip_group_check=True), s_den if d > lo else None)
            dnf = dn[:, lo:lo + 2, :].rearrange("p t c -> p (t c)")
            m0 = put("dve", [m], lambda: V.tensor_scalar(dnf, bd[:, 2 * lo:2 * lo + 4], EPS, None, ALU.add), s_dn)
            dn_m[lo] = put("dve", [m0], lambda: V.reciprocal(dnf, dnf), s_dn)
            ring["rel"][kd] = m0

        dn_m = {}
        def residual(d, i):
            ob, lo, hi = D_pieces(d)[i]
            r_m[d, i] = put("dve", [D_m[d, i], dn_m[2 * (d // 2)], m_xb, hl_m[H, d]], lambda: V.scalar_tensor_tensor(
                out=res[:, d, lo:hi], in0=ob, scalar=dn[:, d, 0:1], in1=xr[:, d, lo:hi], op0=ALU.mult, op1=ALU.add), s_res)
            if i:
                mr_m[d] = r_m[d, i]

        def stats(d, i):
            lo, hi = D_pieces(d)[i][1:]
            return put("dve", [r_m[d, i]], lambda: V.bn_stats(st6[:, d, i, :], res[:, d, lo:hi]), s_st)

        r_m = {}
        for t in range(NT):
            if t == NT - 1:
                tail_denom(0)
            for d in range(2):
                for i in range(2):
                    stage_D(d, t, i)
        residual(0, 0)
        stats(0, 0)
        residual(0, 1)
        for d in range(NT):
            if d + 1 < NT:
                if d:
                    for i in range(2):
                        for t in range(NT):
                            stage_D(d + 1, t, i)
                            if d == 1 and i == 0 and t == 2:
                                tail_denom(2)
                residual(d + 1, 0)
            ms = stats(d, 1)
            if d + 1 < NT:
                stats(d + 1, 0)
            mm = put("dve", [ms], lambda d=d: V.bn_aggr(mv[:, d, :], st6[:, d, :, :]), s_mv)
            m1 = put("act", [mm, m_eps, m_sq], lambda d=d: A.activation(rs[:, d, 0:1], mv[:, d, 1:2], ACT.Sqrt, bias=epc[:, :]), s_rs)
            if d + 1 < NT:
                residual(d + 1, 1)
            m2 = put("dve", [m1], lambda d=d: V.reciprocal(rs[:, d, 1:2], rs[:, d, 0:1]), s_mv)
            if d < NT - 1:
                mn = put("dve", [m2], lambda d=d: V.scalar_tensor_tensor(
                    out=rs[:, d, 0:1], in0=mv[:, d, 0:1], scalar=-1.0, in1=rs[:, d, 1:2], op0=ALU.mult, op1=ALU.mult), s_mv)
                mf = [put("act", [mn], lambda d=d: A.activation(
                    res[:, d, :], res[:, d, :], ACT.Identity, bias=rs[:, d, 0:1], scale=rs[:, d, 1:2]), s_rs)]
            else:
                mf = [put("dve", [m2], lambda d=d: V.tensor_scalar(
                    res[:, d, :], res[:, d, :], mv[:, d, 0:1], rs[:, d, 1:2], ALU.subtract, ALU.mult), s_fin)]
            last = put("sp", mf, lambda d=d: S.dma_start(outv[:, d, :], res[:, d, :]), s_out, 16)
        queue["sp"].append(lambda e: e.wait_ge(last[0][1], last[1]))

        with nc.Block() as block:
            def run(name):
                def body(e):
                    for step in queue[name]:
                        step(e)
                return body
            block.sync(run("sp"))
            block.scalar(run("act"))
            block.vector(run("dve"))
            block.gpsimd(run("pool"))
            block.tensor(run("pe"))


def kernel(**inputs):
    import numpy as np
    import concourse.bacc as bacc
    from concourse import mybir as mb
    from concourse.bass_utils import run_bass_kernel_spmd

    nc = bacc.Bacc("TRN2", target_bir_lowering=False, num_devices=1)
    p = "L0_gnn_"
    x = np.asarray(inputs["x"])
    b1 = np.asarray(inputs[p + "b1"])
    given = [("x", x), ("xT", x.T), ("src", inputs["src"]), ("dst", inputs["dst"]), ("W1", inputs[p + "W1"]),
             ("as1", inputs[p + "a_src1"]), ("ad1", inputs[p + "a_dst1"]), ("b1c", b1.reshape(48, 128).T),
             ("W2", inputs[p + "W2"]), ("as2", inputs[p + "a_src2"]), ("ad2", inputs[p + "a_dst2"]),
             ("b2", inputs[p + "b2"])]
    arrays, args = {}, []
    for name, a in given:
        a = np.ascontiguousarray(np.asarray(a))
        arrays[f"in_{name}"] = a
        args.append(nc.dram_tensor(f"in_{name}", a.shape, mb.dt.from_np(a.dtype), kind="ExternalInput").ap())
    o = nc.dram_tensor("out_0", (512, 768), mb.dt.float32, kind="ExternalOutput").ap()
    gat_resnorm_kernel(nc, *args, o)
    r = run_bass_kernel_spmd(nc, [arrays], core_ids=[0])
    return r.results[0]["out_0"]
```
